# Optimizing a Trainium2 kernel written in Bass

```python
import numpy as np
import jax
import jax.numpy as jnp

def _softmax(x, axis=-1):
    return jax.nn.softmax(x, axis=axis)

def _gelu(x):
    return jax.nn.gelu(x, approximate=True)

def _silu(x):
    return jax.nn.silu(x)

def _sigmoid(x):
    return jax.nn.sigmoid(x)

def _layernorm(x, axis=-1, eps=1e-05):
    m = jnp.mean(x, axis=axis, keepdims=True)
    v = jnp.var(x, axis=axis, keepdims=True)
    return (x - m) / jnp.sqrt(v + eps)

def _scatter_add(tgt, idx, src, axis=0):
    return tgt.at[idx].add(src)

def _segment_sum(src, seg, n):
    return jax.ops.segment_sum(src, seg, n)
kernel_name = 'mk_conv_seq_d4_conv_nchw1024_r2_4e3dc0'

def setup_inputs(seed: int=0):
    np.random.seed(seed)
    _w = jnp.asarray

    def _rec_inputs():
        import jax
        import jax.numpy as jnp
        _gk = jax.random.key(seed)
        x = -0.0003929 + 0.9999 * jax.random.normal(jax.random.fold_in(_gk, 1), (4, 512, 32, 32), jnp.float32)
        return x
    x = _rec_inputs()

    def _L0_conv_setup():
        import jax, jax.numpy as jnp
        import numpy as np
        B, CIN, CB, H, W = (4, 512, 128, 32, 32)
        PAD, DIL = (1, 1)

        def _bn(y, s, b):
            return y * s[None, :, None, None] + b[None, :, None, None]

        def _deform_conv3x3(x, offset, weight):
            Bn, C, Hh, Ww = x.shape
            KK = 9
            off = offset.reshape(Bn, KK, 2, Hh, Ww)
            iy = jnp.repeat(jnp.arange(3), 3).astype(x.dtype)
            jx = jnp.tile(jnp.arange(3), 3).astype(x.dtype)
            hs = jnp.arange(Hh, dtype=x.dtype) - PAD
            ws = jnp.arange(Ww, dtype=x.dtype) - PAD
            ys = off[:, :, 0] + hs[None, None, :, None] + (iy * DIL)[None, :, None, None]
            xs = off[:, :, 1] + ws[None, None, None, :] + (jx * DIL)[None, :, None, None]
            y0 = jnp.floor(ys)
            x0 = jnp.floor(xs)
            xf = x.reshape(Bn, C, Hh * Ww)

            def gather(yy, xx, wgt):
                valid = (yy >= 0) & (yy <= Hh - 1) & (xx >= 0) & (xx <= Ww - 1)
                yi = jnp.clip(yy, 0, Hh - 1).astype(jnp.int32)
                xi = jnp.clip(xx, 0, Ww - 1).astype(jnp.int32)
                idx = (yi * Ww + xi).reshape(Bn, 1, -1)
                v = jnp.take_along_axis(xf, idx, axis=2)
                w = (wgt * valid.astype(x.dtype)).reshape(Bn, 1, -1)
                return v * w
            samp = gather(y0, x0, (y0 + 1 - ys) * (x0 + 1 - xs)) + gather(y0, x0 + 1, (y0 + 1 - ys) * (xs - x0)) + gather(y0 + 1, x0, (ys - y0) * (x0 + 1 - xs)) + gather(y0 + 1, x0 + 1, (ys - y0) * (xs - x0))
            samp = samp.reshape(Bn, C, KK, Hh, Ww)
            return jnp.einsum('ock,bckhw->bohw', weight.reshape(weight.shape[0], C, KK), samp)
        key = jax.random.key(seed)
        ks = jax.random.split(key, 6)
        f = jax.random.normal
        return {'x': f(ks[0], (B, CIN, H, W), jnp.float32), 'conv1_w': f(ks[1], (CB, CIN, 1, 1), jnp.float32) * 0.02, 'bn1_s': jnp.ones((CB,), jnp.float32), 'bn1_b': jnp.zeros((CB,), jnp.float32), 'off_w': f(ks[2], (18, CB, 3, 3), jnp.float32) * 0.01, 'off_b': jnp.zeros((18,), jnp.float32), 'conv2_w': f(ks[3], (CB, CB, 3, 3), jnp.float32) * 0.02, 'bn2_s': jnp.ones((CB,), jnp.float32), 'bn2_b': jnp.zeros((CB,), jnp.float32), 'conv3_w': f(ks[4], (CIN, CB, 1, 1), jnp.float32) * 0.02, 'bn3_s': jnp.ones((CIN,), jnp.float32), 'bn3_b': jnp.zeros((CIN,), jnp.float32)}
    _L0_conv_all = _L0_conv_setup()
    _L0_conv_in = {k: v for k, v in _L0_conv_all.items() if k in ('conv1_w', 'bn1_s', 'bn1_b', 'off_w', 'off_b', 'conv2_w', 'bn2_s', 'bn2_b', 'conv3_w', 'bn3_s', 'bn3_b')}
    del _L0_conv_all

    def _L1_conv_setup():
        import jax, jax.numpy as jnp
        import numpy as np
        KERNEL_SIZE = 5
        EPS = 1e-06

        def local_self_correlation(x, k):
            pad = k // 2
            b, c, h, w = x.shape
            xp = jnp.pad(x, ((0, 0), (0, 0), (pad, pad), (pad, pad)))
            outs = []
            for dy in range(-pad, pad + 1):
                for dx in range(-pad, pad + 1):
                    nb = xp[:, :, pad + dy:pad + dy + h, pad + dx:pad + dx + w]
                    outs.append(jnp.sum(nb * x, axis=1))
            return jnp.stack(outs, axis=1)

        def feature_l2norm(f):
            norm = jnp.sqrt(jnp.sum(f * f, axis=1, keepdims=True) + EPS)
            return f / norm
        key = jax.random.key(seed)
        k1, k2, k3 = jax.random.split(key, 3)
        b, c, h, w = (8, 512, 32, 32)
        hidden = 512
        in_dim = c + KERNEL_SIZE * KERNEL_SIZE
        x = jax.random.normal(k1, (b, c, h, w), dtype=jnp.float32)
        W = jax.random.normal(k2, (hidden, in_dim), dtype=jnp.float32) * 0.02
        bias = jax.random.normal(k3, (hidden,), dtype=jnp.float32) * 0.02
        return {'x': x, 'W': W, 'b': bias}
    _L1_conv_all = _L1_conv_setup()
    _L1_conv_in = {k: v for k, v in _L1_conv_all.items() if k in ('W', 'b')}
    del _L1_conv_all

    def _L2_conv_setup():
        import jax, jax.numpy as jnp
        import numpy as np
        EPS = 1e-05

        def _conv(x, w, stride=1, padding=0):
            return jax.lax.conv_general_dilated(x, w, window_strides=(stride, stride), padding=((padding, padding), (padding, padding)), dimension_numbers=('NCHW', 'OIHW', 'NCHW'))

        def _bn(x, gamma, beta, mean, var):
            inv = gamma / jnp.sqrt(var + EPS)
            return x * inv[None, :, None, None] + (beta - mean * inv)[None, :, None, None]
        key = jax.random.key(seed)
        ks = jax.random.split(key, 16)
        B, Cin, H, W = (32, 512, 28, 28)
        width, Cout = (128, 512)
        d = {}
        d['x'] = jax.random.normal(ks[0], (B, Cin, H, W), jnp.float32)
        d['w1'] = jax.random.normal(ks[1], (width, Cin, 1, 1), jnp.float32) * 0.03
        d['w2'] = jax.random.normal(ks[2], (width, width, 3, 3), jnp.float32) * 0.02
        d['w3'] = jax.random.normal(ks[3], (Cout, width, 1, 1), jnp.float32) * 0.03
        for i, c in [(1, width), (2, width), (3, Cout)]:
            d[f'g{i}'] = jnp.ones((c,), jnp.float32)
            d[f'b{i}'] = jnp.zeros((c,), jnp.float32)
            d[f'm{i}'] = jax.random.normal(ks[4 + i], (c,), jnp.float32) * 0.1
            d[f'v{i}'] = jax.random.uniform(ks[8 + i], (c,), jnp.float32, 0.5, 1.5)
        return d
    _L2_conv_all = _L2_conv_setup()
    _L2_conv_in = {k: v for k, v in _L2_conv_all.items() if k in ('w1', 'w2', 'w3', 'g1', 'b1', 'm1', 'v1', 'g2', 'b2', 'm2', 'v2', 'g3', 'b3', 'm3', 'v3')}
    del _L2_conv_all

    def _L3_conv_setup():
        import jax, jax.numpy as jnp
        import numpy as np
        DN = ('NCHW', 'OIHW', 'NCHW')

        def _conv(x, w, padding):
            return jax.lax.conv_general_dilated(x, w, window_strides=(1, 1), padding=padding, dimension_numbers=DN)

        def _scale_bias(y, s, b):
            return y * s[None, :, None, None] + b[None, :, None, None]
        key = jax.random.key(seed)
        ks = jax.random.split(key, 10)
        N, Cin, H, W = (32, 512, 32, 32)
        Cb, Cout = (128, 512)
        x = jax.random.normal(ks[0], (N, Cin, H, W), dtype=jnp.float32)
        w1 = jax.random.normal(ks[1], (Cb, Cin, 1, 1), dtype=jnp.float32) * 0.02
        w2 = jax.random.normal(ks[2], (Cb, Cb, 3, 3), dtype=jnp.float32) * 0.02
        w3 = jax.random.normal(ks[3], (Cout, Cb, 1, 1), dtype=jnp.float32) * 0.02
        scale1 = jax.random.uniform(ks[4], (Cb,), dtype=jnp.float32, minval=0.5, maxval=1.5)
        bias1 = jax.random.normal(ks[5], (Cb,), dtype=jnp.float32) * 0.1
        scale2 = jax.random.uniform(ks[6], (Cb,), dtype=jnp.float32, minval=0.5, maxval=1.5)
        bias2 = jax.random.normal(ks[7], (Cb,), dtype=jnp.float32) * 0.1
        scale3 = jax.random.uniform(ks[8], (Cout,), dtype=jnp.float32, minval=0.5, maxval=1.5)
        bias3 = jax.random.normal(ks[9], (Cout,), dtype=jnp.float32) * 0.1
        return {'x': x, 'w1': w1, 'w2': w2, 'w3': w3, 'scale1': scale1, 'bias1': bias1, 'scale2': scale2, 'bias2': bias2, 'scale3': scale3, 'bias3': bias3}
    _L3_conv_all = _L3_conv_setup()
    _L3_conv_in = {k: v for k, v in _L3_conv_all.items() if k in ('w1', 'w2', 'w3', 'scale1', 'bias1', 'scale2', 'bias2', 'scale3', 'bias3')}
    del _L3_conv_all
    return {'x': x, 'L0_conv_conv1_w': _L0_conv_in['conv1_w'], 'L0_conv_bn1_s': _L0_conv_in['bn1_s'], 'L0_conv_bn1_b': _L0_conv_in['bn1_b'], 'L0_conv_off_w': _L0_conv_in['off_w'], 'L0_conv_off_b': _L0_conv_in['off_b'], 'L0_conv_conv2_w': _L0_conv_in['conv2_w'], 'L0_conv_bn2_s': _L0_conv_in['bn2_s'], 'L0_conv_bn2_b': _L0_conv_in['bn2_b'], 'L0_conv_conv3_w': _L0_conv_in['conv3_w'], 'L0_conv_bn3_s': _L0_conv_in['bn3_s'], 'L0_conv_bn3_b': _L0_conv_in['bn3_b'], 'L1_conv_W': _L1_conv_in['W'], 'L1_conv_b': _L1_conv_in['b'], 'L2_conv_w1': _L2_conv_in['w1'], 'L2_conv_w2': _L2_conv_in['w2'], 'L2_conv_w3': _L2_conv_in['w3'], 'L2_conv_g1': _L2_conv_in['g1'], 'L2_conv_b1': _L2_conv_in['b1'], 'L2_conv_m1': _L2_conv_in['m1'], 'L2_conv_v1': _L2_conv_in['v1'], 'L2_conv_g2': _L2_conv_in['g2'], 'L2_conv_b2': _L2_conv_in['b2'], 'L2_conv_m2': _L2_conv_in['m2'], 'L2_conv_v2': _L2_conv_in['v2'], 'L2_conv_g3': _L2_conv_in['g3'], 'L2_conv_b3': _L2_conv_in['b3'], 'L2_conv_m3': _L2_conv_in['m3'], 'L2_conv_v3': _L2_conv_in['v3'], 'L3_conv_w1': _L3_conv_in['w1'], 'L3_conv_w2': _L3_conv_in['w2'], 'L3_conv_w3': _L3_conv_in['w3'], 'L3_conv_scale1': _L3_conv_in['scale1'], 'L3_conv_bias1': _L3_conv_in['bias1'], 'L3_conv_scale2': _L3_conv_in['scale2'], 'L3_conv_bias2': _L3_conv_in['bias2'], 'L3_conv_scale3': _L3_conv_in['scale3'], 'L3_conv_bias3': _L3_conv_in['bias3']}

def reference(x, L0_conv_conv1_w, L0_conv_bn1_s, L0_conv_bn1_b, L0_conv_off_w, L0_conv_off_b, L0_conv_conv2_w, L0_conv_bn2_s, L0_conv_bn2_b, L0_conv_conv3_w, L0_conv_bn3_s, L0_conv_bn3_b, L1_conv_W, L1_conv_b, L2_conv_w1, L2_conv_w2, L2_conv_w3, L2_conv_g1, L2_conv_b1, L2_conv_m1, L2_conv_v1, L2_conv_g2, L2_conv_b2, L2_conv_m2, L2_conv_v2, L2_conv_g3, L2_conv_b3, L2_conv_m3, L2_conv_v3, L3_conv_w1, L3_conv_w2, L3_conv_w3, L3_conv_scale1, L3_conv_bias1, L3_conv_scale2, L3_conv_bias2, L3_conv_scale3, L3_conv_bias3):
    import jax
    import jax.numpy as jnp

    def _L0_conv_ref(x, conv1_w, bn1_s, bn1_b, off_w, off_b, conv2_w, bn2_s, bn2_b, conv3_w, bn3_s, bn3_b):
        import jax, jax.numpy as jnp
        import numpy as np
        B, CIN, CB, H, W = (4, 512, 128, 32, 32)
        PAD, DIL = (1, 1)

        def _bn(y, s, b):
            return y * s[None, :, None, None] + b[None, :, None, None]

        def _deform_conv3x3(x, offset, weight):
            Bn, C, Hh, Ww = x.shape
            KK = 9
            off = offset.reshape(Bn, KK, 2, Hh, Ww)
            iy = jnp.repeat(jnp.arange(3), 3).astype(x.dtype)
            jx = jnp.tile(jnp.arange(3), 3).astype(x.dtype)
            hs = jnp.arange(Hh, dtype=x.dtype) - PAD
            ws = jnp.arange(Ww, dtype=x.dtype) - PAD
            ys = off[:, :, 0] + hs[None, None, :, None] + (iy * DIL)[None, :, None, None]
            xs = off[:, :, 1] + ws[None, None, None, :] + (jx * DIL)[None, :, None, None]
            y0 = jnp.floor(ys)
            x0 = jnp.floor(xs)
            xf = x.reshape(Bn, C, Hh * Ww)

            def gather(yy, xx, wgt):
                valid = (yy >= 0) & (yy <= Hh - 1) & (xx >= 0) & (xx <= Ww - 1)
                yi = jnp.clip(yy, 0, Hh - 1).astype(jnp.int32)
                xi = jnp.clip(xx, 0, Ww - 1).astype(jnp.int32)
                idx = (yi * Ww + xi).reshape(Bn, 1, -1)
                v = jnp.take_along_axis(xf, idx, axis=2)
                w = (wgt * valid.astype(x.dtype)).reshape(Bn, 1, -1)
                return v * w
            samp = gather(y0, x0, (y0 + 1 - ys) * (x0 + 1 - xs)) + gather(y0, x0 + 1, (y0 + 1 - ys) * (xs - x0)) + gather(y0 + 1, x0, (ys - y0) * (x0 + 1 - xs)) + gather(y0 + 1, x0 + 1, (ys - y0) * (xs - x0))
            samp = samp.reshape(Bn, C, KK, Hh, Ww)
            return jnp.einsum('ock,bckhw->bohw', weight.reshape(weight.shape[0], C, KK), samp)
        relu = jax.nn.relu
        out = jnp.einsum('oc,bchw->bohw', conv1_w[:, :, 0, 0], x)
        out = relu(_bn(out, bn1_s, bn1_b))
        offset = jax.lax.conv_general_dilated(out, off_w, (1, 1), [(PAD, PAD), (PAD, PAD)], rhs_dilation=(DIL, DIL), dimension_numbers=('NCHW', 'OIHW', 'NCHW')) + off_b[None, :, None, None]
        out = _deform_conv3x3(out, offset, conv2_w)
        out = relu(_bn(out, bn2_s, bn2_b))
        out = jnp.einsum('oc,bchw->bohw', conv3_w[:, :, 0, 0], out)
        out = _bn(out, bn3_s, bn3_b)
        return relu(out + x)

    def _L1_conv_ref(x, W, b):
        import jax, jax.numpy as jnp
        import numpy as np
        KERNEL_SIZE = 5
        EPS = 1e-06

        def local_self_correlation(x, k):
            pad = k // 2
            b, c, h, w = x.shape
            xp = jnp.pad(x, ((0, 0), (0, 0), (pad, pad), (pad, pad)))
            outs = []
            for dy in range(-pad, pad + 1):
                for dx in range(-pad, pad + 1):
                    nb = xp[:, :, pad + dy:pad + dy + h, pad + dx:pad + dx + w]
                    outs.append(jnp.sum(nb * x, axis=1))
            return jnp.stack(outs, axis=1)

        def feature_l2norm(f):
            norm = jnp.sqrt(jnp.sum(f * f, axis=1, keepdims=True) + EPS)
            return f / norm
        feature_gs = local_self_correlation(x, KERNEL_SIZE)
        feature_gs = feature_l2norm(feature_gs)
        feature_cat = jnp.concatenate([x, feature_gs], axis=1)
        out = jnp.einsum('bihw,oi->bohw', feature_cat, W) + b[None, :, None, None]
        return jax.nn.relu(out)

    def _L2_conv_ref(x, w1, w2, w3, g1, b1, m1, v1, g2, b2, m2, v2, g3, b3, m3, v3):
        import jax, jax.numpy as jnp
        import numpy as np
        EPS = 1e-05

        def _conv(x, w, stride=1, padding=0):
            return jax.lax.conv_general_dilated(x, w, window_strides=(stride, stride), padding=((padding, padding), (padding, padding)), dimension_numbers=('NCHW', 'OIHW', 'NCHW'))

        def _bn(x, gamma, beta, mean, var):
            inv = gamma / jnp.sqrt(var + EPS)
            return x * inv[None, :, None, None] + (beta - mean * inv)[None, :, None, None]
        out = jax.nn.relu(_bn(_conv(x, w1), g1, b1, m1, v1))
        out = jax.nn.relu(_bn(_conv(out, w2, stride=1, padding=1), g2, b2, m2, v2))
        out = _bn(_conv(out, w3), g3, b3, m3, v3)
        return jax.nn.relu(out + x)

    def _L3_conv_ref(x, w1, w2, w3, scale1, bias1, scale2, bias2, scale3, bias3):
        import jax, jax.numpy as jnp
        import numpy as np
        DN = ('NCHW', 'OIHW', 'NCHW')

        def _conv(x, w, padding):
            return jax.lax.conv_general_dilated(x, w, window_strides=(1, 1), padding=padding, dimension_numbers=DN)

        def _scale_bias(y, s, b):
            return y * s[None, :, None, None] + b[None, :, None, None]
        out1 = jax.nn.relu(_scale_bias(_conv(x, w1, 'VALID'), scale1, bias1))
        out2 = jax.nn.relu(_scale_bias(_conv(out1, w2, ((1, 1), (1, 1))), scale2, bias2))
        out = jax.nn.relu(_scale_bias(_conv(out2, w3, 'VALID'), scale3, bias3) + x)
        return out

    def _gn(v, G=32, eps=1e-05):
        B_, C_, H_, W_ = v.shape
        g = v.reshape(B_, G, C_ // G, H_, W_)
        m = jnp.mean(g, axis=(2, 3, 4), keepdims=True)
        s = jnp.var(g, axis=(2, 3, 4), keepdims=True)
        return ((g - m) / jnp.sqrt(s + eps)).reshape(v.shape)

    def _ln_c(v, eps=1e-06):
        m = jnp.mean(v, axis=1, keepdims=True)
        s = jnp.var(v, axis=1, keepdims=True)
        return (v - m) / jnp.sqrt(s + eps)

    def _ln_t(v, eps=1e-05):
        m = jnp.mean(v, axis=-1, keepdims=True)
        s = jnp.var(v, axis=-1, keepdims=True)
        return (v - m) / jnp.sqrt(s + eps)

    def _to_tokens(v):
        B_, C_, H_, W_ = v.shape
        return v.reshape(B_, C_, H_ * W_).transpose(0, 2, 1)

    def _from_tokens(t, like):
        B_, C_, H_, W_ = like.shape
        return t.transpose(0, 2, 1).reshape(B_, C_, H_, W_)
    x = _L0_conv_ref(x, L0_conv_conv1_w, L0_conv_bn1_s, L0_conv_bn1_b, L0_conv_off_w, L0_conv_off_b, L0_conv_conv2_w, L0_conv_bn2_s, L0_conv_bn2_b, L0_conv_conv3_w, L0_conv_bn3_s, L0_conv_bn3_b)
    x = _L1_conv_ref(x, L1_conv_W, L1_conv_b)
    x = _L2_conv_ref(x, L2_conv_w1, L2_conv_w2, L2_conv_w3, L2_conv_g1, L2_conv_b1, L2_conv_m1, L2_conv_v1, L2_conv_g2, L2_conv_b2, L2_conv_m2, L2_conv_v2, L2_conv_g3, L2_conv_b3, L2_conv_m3, L2_conv_v3)
    x = _L3_conv_ref(x, L3_conv_w1, L3_conv_w2, L3_conv_w3, L3_conv_scale1, L3_conv_bias1, L3_conv_scale2, L3_conv_bias2, L3_conv_scale3, L3_conv_bias3)
    return x

_drawn_inputs = setup_inputs


def setup_inputs(seed=0):
    import zlib

    import numpy as np

    out = dict(_drawn_inputs(seed))
    spreads = {'L0_conv_bn1_s': (1.0, 0.6),
     'L0_conv_bn1_b': (0.0, 0.8),
     'L0_conv_off_b': (0.0, 0.8),
     'L0_conv_bn2_s': (1.0, 0.6),
     'L0_conv_bn2_b': (0.0, 0.687),
     'L0_conv_bn3_s': (1.0, 0.6),
     'L0_conv_bn3_b': (0.0, 0.1),
     'L2_conv_g1': (1.0, 0.6),
     'L2_conv_b1': (0.0, 0.297),
     'L2_conv_g2': (1.0, 0.6),
     'L2_conv_b2': (0.0, 0.1),
     'L2_conv_g3': (1.0, 0.2),
     'L2_conv_b3': (0.0, 0.1)}
    factors = {'L0_conv_conv1_w': 3.639,
     'L0_conv_off_w': 8.0,
     'L0_conv_conv2_w': 2.813,
     'L2_conv_v1': 4.867,
     'L2_conv_v2': 3.359,
     'L3_conv_scale1': 7.14,
     'L3_conv_scale2': 5.824,
     'L3_conv_scale3': 3.931}
    for name, (base, spread) in spreads.items():
        noise = np.random.default_rng([zlib.crc32(name.encode()), seed]).standard_normal(out[name].shape)
        drawn = base * np.exp(spread * noise) if base else spread * noise
        out[name] = jnp.asarray(drawn.astype(out[name].dtype))
    for name, factor in factors.items():
        out[name] = (out[name] * factor).astype(out[name].dtype)
    return out
```

```python
import concourse.bass as bass
from concourse import mybir
from contextlib import ExitStack

N, C, H, W = 4, 512, 32, 32
P = 128
HW = H * W
KC = C // P
HALF = HW // 2
TAPS = 9
TILES = HW // P
RT = P // W
HT = TILES // 2
HR = H // 2
KS = 5
PADK = KS // 2
NB = KS * KS
FOLD = 8
ENTRY = W + 1
TABLE = HW + ENTRY
UNITS = 2 * TAPS
SLOTS = 8
BLEND = 4 * HT
L1_EPS = 1e-6
BN_EPS = 1e-5

L0_S1, L0_B1, L0_S2, L0_B2, L0_S3, L0_B3 = 0, 1, 2, 3, 4, 8
L1_B = 12
L2_G, L2_B, L2_M, L2_V = 16, 22, 28, 34
L3_S1, L3_B1, L3_S2, L3_B2, L3_S3, L3_B3 = 40, 41, 42, 43, 44, 48
NPAR = 52

C_STEPS = ([("gram", g) for g in range(4)] + [("corrT", 0)] + [("mix", 0, m) for m in range(KC)]
           + [("corrT", 1)] + [("mix", 1, m) for m in range(KC)])
for layer in (2, 3):
    C_STEPS += [("reduce", layer, 0), ("reduce", layer, 1), ("conv", layer, 0), ("conv", layer, 1)]
    C_STEPS += [("expand", layer, h, m) for h in range(2) for m in range(KC)]
NC = len(C_STEPS)
C_BANKS = 4


def build_schedule():
    units = {}
    u = 0
    for name, take in (("gram", 4), ("mix", 8), ("reduce2", 2), ("conv2", 2), ("reduce3", 2)):
        n = 0
        for c, s in enumerate(C_STEPS):
            key = s[0] + (str(s[1]) if s[0] in ("reduce", "conv") else "")
            if key == name and n < take:
                units[c] = u
                u, n = u + 1, n + 1
    assert u == UNITS
    expands = {}
    at = [c for c, s in enumerate(C_STEPS) if s[:2] == ("conv", 2)]
    at += [c for c, s in enumerate(C_STEPS) if s[:2] == ("conv", 3)]
    for i, c in enumerate(at):
        expands[c] = [(i // 2, 2 * (i % 2) + j) for j in range(2)]
    items = [("blend", 0, 0), ("blend", 0, 1)]
    for c in range(NC):
        items.append(("step", c))
        if c in units:
            u = units[c]
            items.append(("turn", u))
            if u + 1 < UNITS:
                items += [("blend", u + 1, 0), ("blend", u + 1, 1)]
            if u:
                items.append(("tap", u - 1))
            if u == UNITS - 1:
                items.append(("tap", u))
        for h, m in expands.get(c, ()):
            items.append(("out0", h, m))
    return items


SCHEDULE = build_schedule()
B_ONLY = [it for it in SCHEDULE if it[0] != "step"]
C_ONLY = [it for it in SCHEDULE if it[0] == "step"]
BANK_USES = [len([c for c in range(NC) if c % C_BANKS == b]) for b in range(C_BANKS)]
STEP_AT = {s: c for c, s in enumerate(C_STEPS)}


def drains(ic, c):
    return ic * BANK_USES[c % C_BANKS] + c // C_BANKS


def wait_past(eng, sem, value):
    if not (isinstance(value, int) and value <= 0):
        eng.wait_ge(sem, value)


def conv_seq_kernel(nc, x, w1t, offwt, offb, w2t, w3t, l1wt, l1gt, l2w1t, l2w2t, l2w3t, l3w1t, l3w2t, l3w3t,
                    par, out):
    fp32 = mybir.dt.float32
    i32 = mybir.dt.int32
    ALU = mybir.AluOpType
    ACT = mybir.ActivationFunctionType
    AX = mybir.AxisListType

    x_v = x.rearrange("n (k p) a b -> n p k (a b)", p=P)
    out_v = out.rearrange("n (k p) a b -> n k p (a b)", p=P)
    table = nc.dram_tensor("patch_table", (N * TABLE, 4 * P), fp32, kind="Internal").ap()
    table_v = table.rearrange("(n e) c -> n e c", e=TABLE)

    ctx = ExitStack()
    with ctx:
        def sb(name, shape, dt=fp32):
            return ctx.enter_context(nc.sbuf_tensor(name, shape, dt))

        def sem(name):
            return ctx.enter_context(nc.semaphore(name))

        w1 = sb("w1", [P, KC, P])
        offw = sb("offw", [P, TAPS, 2 * TAPS])
        offb_t = sb("offb_t", [P, 2 * TAPS])
        w2 = sb("w2", [P, TAPS, P])
        w3 = sb("w3", [P, C])
        l1w = sb("l1w", [P, KC, C])
        l1g = sb("l1g", [NB, C])
        wr = {2: sb("l2w1", [P, KC, P]), 3: sb("l3w1", [P, KC, P])}
        wc = {2: sb("l2w2", [P, TAPS, P]), 3: sb("l3w2", [P, TAPS, P])}
        we = {2: sb("l2w3", [P, C]), 3: sb("l3w3", [P, C])}
        prm = sb("prm", [P, NPAR])
        bn = sb("bn", [P, 4, 6])
        ident = sb("ident", [P, P])

        xa = [sb(f"xa{u}", [P, KC, HW]) for u in range(2)]
        mid = [sb(f"mid{u}", [P, 3, H + 2, W]) for u in range(2)]
        midT = [sb(f"midT{u}", [P, TILES, P]) for u in range(2)]
        grid_i = sb("grid_i", [P, TILES, TAPS, 2], i32)
        grid = sb("grid", [P, TILES, TAPS, 2])
        pix = sb("pix", [P, 4], i32)
        pixf = sb("pixf", [P, 2])
        pos = sb("pos", [P, TILES * TAPS, 2])
        cell = sb("cell", [P, TILES * TAPS, 2])
        cell_i = sb("cell_i", [P, TILES * TAPS, 2], i32)
        far = sb("far", [P, TILES * TAPS, 2])
        hat = sb("hat", [P, 2, TILES * TAPS, 2])
        entry = sb("entry", [P, TILES * TAPS])
        first_entry = sb("first_entry", [P, 1])
        idx_all = sb("idx_all", [P, N, TILES * TAPS], i32)
        wgt_all = sb("wgt_all", [P, N, TILES * TAPS, 4])
        tick = sb("tick", [1, 1 + 2 * UNITS])
        idx = sb("idx", [P, TILES * TAPS], i32)
        wgt = sb("wgt", [P, TILES * TAPS, 4])
        patch = sb("patch", [P, SLOTS, 4, P])
        samp = sb("samp", [P, 2, HT, P])
        sampT = sb("sampT", [P, 2, HALF])
        hid = sb("hid", [P, 2, HALF])
        res = sb("res", [P, KC, HALF])
        x1 = sb("x1", [P, KC, H + 2 * PADK, W])
        col_i = sb("col_i", [P, KS, FOLD], i32)
        band = sb("band", [P, W])
        wide = sb("wide", [P, W])
        pick = sb("pick", [P, KS, FOLD])
        corr = sb("corr", [P, HT, KS, W])
        folded = sb("folded", [P, HT * KS, FOLD])
        picked = sb("picked", [P, HT * KS, KS, FOLD])
        gs = sb("gs", [P, 2, HT, NB])
        gsq = sb("gsq", [P, HT, NB])
        nrm = sb("nrm", [P, 2, 3, HT])
        gsT = sb("gsT", [NB, 2, HALF])
        xs = sb("xs", [P, KC, HW])
        hp = sb("hp", [P, H + 2, W + 2])
        h2 = sb("h2", [P, HW])

        bank = [ctx.enter_context(nc.psum_tensor(f"bank{b}", [P, HALF], fp32)) for b in range(8)]

        ld_first, ld_deform, ld_late = sem("ld_first"), sem("ld_deform"), sem("ld_late")
        ld_xa = [sem(f"ld_xa{u}") for u in range(2)]
        iota_done, const_done, borders_done = sem("iota_done"), sem("const_done"), sem("borders_done")
        root_asked, root_done, bn_done = sem("root_asked"), sem("root_done"), sem("bn_done")
        a_conv, a_mid, a_turn, a_midT, a_off = (sem(s) for s in ("a_conv", "a_mid", "a_turn", "a_midT", "a_off"))
        a_step, a_read = sem("a_step"), sem("a_read")
        tabled = [sem(f"tabled{u}") for u in range(2)]
        taken = sem("taken")
        ticked = sem("ticked")
        zeros_done, filled = sem("zeros_done"), sem("filled")
        gathered = [sem(f"gathered{s}") for s in range(SLOTS)]
        blended = sem("blended")
        turned, sampT_done, tap_done = sem("turned"), sem("sampT_done"), sem("tap_done")
        acc_done, out0_done = sem("acc_done"), sem("out0_done")
        b_drained = [sem(f"b_drained{h}") for h in range(2)]
        ld_res = [sem(f"ld_res{m}") for m in range(KC)]
        x1_done = sem("x1_done")
        c_done = sem("c_done")
        c_drained = [sem(f"c_drained{b}") for b in range(C_BANKS)]
        corr_step, norm_asked, norm_root, gs_done = sem("corr_step"), sem("norm_asked"), sem("norm_root"), sem("gs_done")
        x3_done, y_done = sem("x3_done"), sem("y_done")
        stored = [sem(f"stored{n}") for n in range(2 * KC)]

        block = ctx.enter_context(nc.Block())

        A_STEPS = 19
        HALF_STEPS = 15
        CORR_STEPS = 30

        @block.sync
        def _(sp):
            for t, d in ((w1, w1t), (prm, par), (offw, offwt), (offb_t, offb)):
                sp.dma_start(t[:], d).then_inc(ld_first, 16)
            sp.dma_start(xa[0][:], x_v[0]).then_inc(ld_xa[0], 16)
            sp.dma_start(xa[1][:], x_v[1]).then_inc(ld_xa[1], 16)
            for t, d in ((w2, w2t), (w3, w3t)):
                sp.dma_start(t[:], d).then_inc(ld_deform, 16)
            sp.wait_ge(zeros_done, 1)
            for corner in range(4):
                shift = corner // 2 * W + corner % 2
                for first, last in ((0, ENTRY - shift), (TABLE - shift, TABLE)):
                    if last > first:
                        sp.dma_start(table_v[:, first:last, corner * P:(corner + 1) * P].rearrange("n e c -> e n c"),
                                     samp[0:last - first, 0]).then_inc(filled, 16)

            def write_table(image, j, u):
                for h in range(2):
                    sp.wait_ge(a_midT, 2 * image + h + 1)
                    for dy in range(2):
                        for dx in range(2):
                            first = ENTRY - dy * W - dx + h * HALF
                            dst = table_v[image, first:first + HALF, (2 * dy + dx) * P:(2 * dy + dx + 1) * P]
                            sp.dma_start(dst.rearrange("(t p) c -> p t c", p=P),
                                         midT[u][:, HT * h:HT * h + HT, :]).then_inc(tabled[u], 16)

            for j in range(N // 2):
                for u in range(2):
                    image = 2 * j + u
                    write_table(image, j, u)
                    if j + 1 < N // 2:
                        sp.wait_ge(a_conv, 2 * image + 2)
                        sp.dma_start(xa[u][:], x_v[image + 2]).then_inc(ld_xa[u], 16)
            for t, d in ((l1w, l1wt), (l1g, l1gt), (wr[2], l2w1t), (wc[2], l2w2t), (we[2], l2w3t),
                         (wr[3], l3w1t), (wc[3], l3w2t), (we[3], l3w3t)):
                sp.dma_start(t[:], d).then_inc(ld_late, 16)

            def body(items, ib, ic):
                for it in items:
                    if it[0] == "blend" and it[1] % 9 == 0 and it[2] == 0:
                        h = it[1] // 9
                        for m in range(KC):
                            wait_past(sp, x1_done, 8 * ib + KC * h + m + 1 - KC)
                            sp.dma_start(res[:, m, :], x_v[ib, :, m, h * HALF:(h + 1) * HALF]).then_inc(ld_res[m], 16)
                    if it[0] == "step" and C_STEPS[it[1]][:2] == ("expand", 3):
                        _, _, h, m = C_STEPS[it[1]]
                        n = KC * h + m
                        sp.wait_ge(y_done, 8 * ic + n + 1)
                        sp.dma_start(out_v[ic, m, :, h * HALF:(h + 1) * HALF],
                                     xs[:, m, h * HALF:(h + 1) * HALF]).then_inc(stored[n], 16)

            body(B_ONLY, 0, 0)
            with sp.Fori(1, N) as i:
                body(SCHEDULE, i, i - 1)
            body(C_ONLY, N, N - 1)
            for n in range(2 * KC):
                sp.wait_ge(stored[n], 16 * N)

        @block.gpsimd
        def _(pool):
            pool.memset(samp[:, 0], 0.0).then_inc(zeros_done, 1)
            pool.iota(pix[:, 0:1], [[0, 1]], base=0, channel_multiplier=1).then_inc(iota_done, 1)
            pool.iota(grid_i[:, :, :, 0].rearrange("p t (a b) -> p t a b", b=3), [[RT, TILES], [1, 3], [0, 3]],
                      base=-1, channel_multiplier=0).then_inc(iota_done, 1)
            pool.iota(grid_i[:, :, :, 1].rearrange("p t (a b) -> p t a b", b=3), [[0, TILES], [0, 3], [1, 3]],
                      base=-1, channel_multiplier=0).then_inc(iota_done, 1)
            pool.iota(col_i[:, :, :], [[1, KS], [-1, FOLD]], base=2 * FOLD - PADK, channel_multiplier=1)\
                .then_inc(iota_done, 1)
            pool.iota(cell_i[:, 0:W, 0], [[1, W]], base=0, channel_multiplier=0).then_inc(iota_done, 1)
            pool.memset(ident[:], 0.0).then_inc(iota_done, 1)
            for u in range(2):
                pool.memset(mid[u][:], 0.0).then_inc(borders_done, 1)
            pool.wait_ge(iota_done, 6)
            pool.affine_select(out=ident[:], in_=ident[:], compare_op=ALU.not_equal, fill=1.0, base=0,
                               pattern=[[-1, P]], channel_multiplier=1).then_inc(const_done, 1)
            pool.memset(hp[:], 0.0).then_inc(borders_done, 1)
            pool.memset(x1[:, :, 0:PADK, :], 0.0).then_inc(borders_done, 1)
            pool.memset(x1[:, :, H + PADK:, :], 0.0).then_inc(borders_done, 1)

            def body(ib):
                wait_past(pool, ticked, 2 * UNITS * ib)
                pool.wait_ge(taken, 2 * ib + 2)
                for u in range(UNITS):
                    h, k = u // TAPS, u % TAPS
                    for t in range(HT):
                        if t % 2 == 0:
                            wait_past(pool, blended, (UNITS * ib + u - SLOTS // HT) * BLEND + 8 * (t // 2) + 8)
                            p = 1 + u * 2 + t // 2
                            pool.tensor_tensor(tick[:, p:p + 1], tick[:, 0:1], tick[:, 0:1], ALU.add).then_inc(ticked, 1)
                        n = HT * u + t
                        e = (HT * h + t) * TAPS + k
                        pool.indirect_dma_start(patch[:, n % SLOTS].rearrange("p a c -> p (a c)"), None, table,
                                                bass.IndirectOffsetOnAxis(ap=idx[:, e:e + 1], axis=0))\
                            .then_inc(gathered[n % SLOTS], 16)

            pool.memset(tick[:], 0.0).then_inc(borders_done, 1)
            pool.wait_ge(borders_done, 6)
            pool.wait_ge(filled, 16 * 6)
            pool.wait_ge(tabled[0], 16 * 8)
            body(0)
            for u in range(2):
                pool.wait_ge(tabled[u], 16 * 8 * (N // 2))
            with pool.Fori(1, N) as i:
                body(i)

        @block.tensor
        def _(pe):
            pe.wait_ge(ld_first, 64)
            pe.wait_ge(const_done, 1)
            with pe.Fori(0, N // 2) as j:
                for u in range(2):
                    image = 2 * j + u
                    pe.wait_ge(ld_xa[u], 16 * j + 16)
                    pe.wait_ge(a_mid, 2 * image)
                    for h in range(2):
                        for k in range(KC):
                            last = pe.matmul(bank[h][:], w1[:, k, :], xa[u][:, k, h * HALF:(h + 1) * HALF],
                                             start=k == 0, stop=k == KC - 1)
                        last.then_inc(a_conv, 1)
                    for h in range(2):
                        pe.wait_ge(a_mid, 2 * image + h + 1)
                        pe.wait_ge(a_midT, 2 * image)
                        for t in range(HT):
                            row = RT * (HT * h + t) + 1
                            last = pe.transpose(bank[2 + h][:, t * P:(t + 1) * P], mid[u][:, 1, row:row + RT, :], ident[:])
                        last.then_inc(a_turn, 1)
                    pe.wait_ge(a_read, image)
                    for t in range(TILES):
                        for k in range(TAPS):
                            row = RT * t + k // 3
                            last = pe.matmul(bank[4][:, t * 2 * TAPS:(t + 1) * 2 * TAPS],
                                             mid[u][:, k % 3, row:row + RT, :], offw[:, k, :],
                                             start=k == 0, stop=k == TAPS - 1)
                    last.then_inc(a_off, 1)

            pe.wait_ge(ld_deform, 32)
            pe.wait_ge(a_midT, 2 * N)
            pe.wait_ge(a_read, N)

            def step(c, ic):
                s = C_STEPS[c]
                ps = bank[c % C_BANKS]
                wait_past(pe, c_drained[c % C_BANKS], drains(ic, c))
                if s[0] == "gram":
                    if s[1] == 0:
                        pe.wait_ge(x1_done, 8 * ic + 8)
                    for half in range(2):
                        t = 2 * s[1] + half
                        for k in range(KC):
                            last = pe.matmul(ps[:, half * 2 * P:(half + 1) * 2 * P],
                                             x1[:, k, RT * t + PADK:RT * t + PADK + RT, :],
                                             x1[:, k, RT * t:RT * t + 2 * RT, :], start=k == 0, stop=k == KC - 1)
                elif s[0] == "corrT":
                    h = s[1]
                    pe.wait_ge(gs_done, 2 * ic + h + 1)
                    for t in range(HT):
                        last = pe.transpose(ps[0:NB, t * P:(t + 1) * P], gs[:, h, t, :], ident[:])
                elif s[0] == "mix":
                    _, h, m = s
                    for k in range(KC):
                        pe.matmul(ps[:], l1w[:, k, m * P:(m + 1) * P],
                                  x1[:, k, PADK + HR * h:PADK + HR * (h + 1), :], start=k == 0, stop=False)
                    ct = STEP_AT[("corrT", h)]
                    pe.wait_ge(c_drained[ct % C_BANKS], drains(ic, ct) + 1)
                    last = pe.matmul(ps[:], l1g[:, m * P:(m + 1) * P], gsT[:, h, :], start=False, stop=True)
                elif s[0] == "reduce":
                    _, layer, h = s
                    if layer == 2:
                        for m in range(KC):
                            cm = STEP_AT[("mix", h, m)]
                            pe.wait_ge(c_drained[cm % C_BANKS], drains(ic, cm) + 1)
                    else:
                        pe.wait_ge(x3_done, 8 * ic + KC * (h + 1))
                    for k in range(KC):
                        last = pe.matmul(ps[:], wr[layer][:, k, :], xs[:, k, h * HALF:(h + 1) * HALF],
                                         start=k == 0, stop=k == KC - 1)
                elif s[0] == "conv":
                    _, layer, h = s
                    for hh in range(2):
                        cr = STEP_AT[("reduce", layer, hh)]
                        pe.wait_ge(c_drained[cr % C_BANKS], drains(ic, cr) + 1)
                    for k in range(TAPS):
                        row, col = HR * h + k // 3, k % 3
                        last = pe.matmul(ps[:], wc[layer][:, k, :], hp[:, row:row + HR, col:col + W],
                                         start=k == 0, stop=k == TAPS - 1)
                elif s[0] == "expand":
                    _, layer, h, m = s
                    cv = STEP_AT[("conv", layer, h)]
                    pe.wait_ge(c_drained[cv % C_BANKS], drains(ic, cv) + 1)
                    last = pe.matmul(ps[:], we[layer][:, m * P:(m + 1) * P], h2[:, h * HALF:(h + 1) * HALF],
                                     start=True, stop=True)
                last.then_inc(c_done, 1)

            def body(items, ib, ic):
                for it in items:
                    if it[0] == "step":
                        step(it[1], ic)
                    elif it[0] == "turn":
                        u = it[1]
                        pe.wait_ge(blended, (UNITS * ib + u + 1) * BLEND)
                        wait_past(pe, sampT_done, UNITS * ib + u - 1)
                        for t in range(HT):
                            last = pe.transpose(bank[4 + u % 2][:, t * P:(t + 1) * P], samp[:, u % 2, t, :], ident[:])
                        last.then_inc(turned, 1)
                    elif it[0] == "tap":
                        u = it[1]
                        h, k = u // TAPS, u % TAPS
                        if k == 0:
                            wait_past(pe, b_drained[h], 5 * ib)
                        pe.wait_ge(sampT_done, UNITS * ib + u + 1)
                        pe.matmul(bank[6 + h][:], w2[:, k, :], sampT[:, u % 2, :],
                                  start=k == 0, stop=k == TAPS - 1).then_inc(tap_done, 1)
                    elif it[0] == "out0":
                        _, h, m = it
                        pe.wait_ge(b_drained[h], 5 * ib + m + 1)
                        pe.matmul(bank[6 + h][:], w3[:, m * P:(m + 1) * P], hid[:, h, :],
                                  start=True, stop=True).then_inc(out0_done, 1)

            body(B_ONLY, 0, 0)
            pe.wait_ge(ld_late, 16 * 8)
            pe.wait_ge(borders_done, 6)
            with pe.Fori(1, N) as i:
                body(SCHEDULE, i, i - 1)
            body(C_ONLY, N, N - 1)

        @block.scalar
        def _(act):
            def col(n):
                return prm[:, n:n + 1]

            act.wait_ge(root_asked, 1)
            act.activation(bn[:, 0, :], bn[:, 1, :], ACT.Sqrt).then_inc(root_done, 1)
            act.wait_ge(borders_done, 2)
            act.wait_ge(ld_first, 64)
            with act.Fori(0, N // 2) as j:
                for u in range(2):
                    image = 2 * j + u
                    for h in range(2):
                        act.wait_ge(a_conv, 2 * image + h + 1)
                        act.wait_ge(a_off, 2 * j)
                        rows = slice(1 + HR * h, 1 + HR * (h + 1))
                        ps = bank[h][:].rearrange("p (a b) -> p a b", b=W)
                        for shift in range(3):
                            lo, hi = max(0, 1 - shift), min(W, W + 1 - shift)
                            last = act.activation(mid[u][:, shift, rows, lo:hi],
                                                  ps[:, :, lo + shift - 1:hi + shift - 1], ACT.Relu,
                                                  bias=col(L0_B1), scale=col(L0_S1))
                        last.then_inc(a_mid, 1)
                    for h in range(2):
                        act.wait_ge(a_turn, 2 * image + h + 1)
                        act.wait_ge(tabled[u], 16 * 8 * j)
                        act.activation(midT[u][:, HT * h:HT * (h + 1), :],
                                       bank[2 + h][:].rearrange("p (t c) -> p t c", c=P), ACT.Copy).then_inc(a_midT, 1)
            act.wait_ge(bn_done, 5)

            def step(c, ic):
                s = C_STEPS[c]
                ps = bank[c % C_BANKS]
                if s[0] == "gram":
                    if s[1] % 2:
                        h = s[1] // 2
                        act.wait_ge(norm_asked, 2 * ic + h + 1)
                        act.activation(nrm[:, h, 1, :], nrm[:, h, 0, :], ACT.Sqrt).then_inc(norm_root, 1)
                    return
                if s[0] == "expand":
                    _, layer, h, m = s
                    n = KC * h + m
                    act.wait_ge(c_drained[c % C_BANKS], drains(ic, c) + 1)
                    v = xs[:, m, h * HALF:(h + 1) * HALF]
                    b = bn[:, 3, 2 + m:3 + m] if layer == 2 else col(L3_B3 + m)
                    act.activation(v, v, ACT.Relu, bias=b).then_inc(x3_done if layer == 2 else y_done, 1)
                    return
                act.wait_ge(c_done, NC * ic + c + 1)
                if s[0] == "corrT":
                    ins = act.activation(gsT[:, s[1], :], ps[0:NB, :], ACT.Copy)
                elif s[0] == "mix":
                    _, h, m = s
                    wait_past(act, stored[KC * h + m], 16 * ic)
                    ins = act.activation(xs[:, m, h * HALF:(h + 1) * HALF], ps[:], ACT.Relu, bias=col(L1_B + m))
                elif s[0] == "reduce":
                    _, layer, h = s
                    sc = bn[:, 2, 0:1] if layer == 2 else col(L3_S1)
                    b = bn[:, 3, 0:1] if layer == 2 else col(L3_B1)
                    ins = act.activation(hp[:, 1 + HR * h:1 + HR * (h + 1), 1:W + 1],
                                         ps[:].rearrange("p (a b) -> p a b", b=W), ACT.Relu, bias=b, scale=sc)
                elif s[0] == "conv":
                    _, layer, h = s
                    sc = bn[:, 2, 1:2] if layer == 2 else col(L3_S2)
                    b = bn[:, 3, 1:2] if layer == 2 else col(L3_B2)
                    ins = act.activation(h2[:, h * HALF:(h + 1) * HALF], ps[:], ACT.Relu, bias=b, scale=sc)
                ins.then_inc(c_drained[c % C_BANKS], 1)

            def body(items, ib, ic):
                for it in items:
                    if it[0] == "step":
                        step(it[1], ic)
                    elif it[0] == "turn":
                        u = it[1]
                        act.wait_ge(turned, UNITS * ib + u + 1)
                        wait_past(act, tap_done, UNITS * ib + u - 1)
                        act.activation(sampT[:, u % 2, :], bank[4 + u % 2][:], ACT.Copy).then_inc(sampT_done, 1)
                    elif it[0] == "tap" and it[1] % TAPS == TAPS - 1:
                        u = it[1]
                        h = u // TAPS
                        act.wait_ge(tap_done, UNITS * ib + u + 1)
                        act.activation(hid[:, h, :], bank[6 + h][:], ACT.Relu, bias=col(L0_B2),
                                       scale=col(L0_S2)).then_inc(b_drained[h], 1)
                    elif it[0] == "out0":
                        _, h, m = it
                        act.wait_ge(b_drained[h], 5 * ib + m + 2)
                        act.activation(x1[:, m, PADK + HR * h:PADK + HR * (h + 1), :],
                                       res[:, m, :].rearrange("p (a b) -> p a b", b=W), ACT.Relu,
                                       bias=col(L0_B3 + m)).then_inc(x1_done, 1)

            body(B_ONLY, 0, 0)
            act.wait_ge(borders_done, 6)
            with act.Fori(1, N) as i:
                body(SCHEDULE, i, i - 1)
            body(C_ONLY, N, N - 1)

        @block.vector
        def _(dve):
            def chain(sem_, base):
                done = [0]

                def link(ins, wait=True):
                    ins.then_inc(sem_, 1)
                    done[0] += 1
                    if wait:
                        dve.wait_ge(sem_, base + done[0])
                return link, done

            link, done = chain(bn_done, 0)
            dve.wait_ge(ld_first, 64)
            dve.tensor_scalar(bn[:, 1, :], prm[:, L2_V:L2_V + 6], BN_EPS, None, ALU.add).then_inc(root_asked, 1)
            dve.wait_ge(root_done, 1)
            dve.wait_ge(root_asked, 1)
            dve.reciprocal(bn[:, 2, :], bn[:, 0, :]).then_inc(root_asked, 1)
            dve.wait_ge(root_asked, 2)
            dve.tensor_tensor(bn[:, 2, :], bn[:, 2, :], bn[:, 1, :], ALU.mult).then_inc(root_asked, 1)
            dve.wait_ge(root_asked, 3)
            link(dve.tensor_tensor(bn[:, 2, :], bn[:, 2, :], bn[:, 0, :], ALU.add))
            link(dve.reciprocal(bn[:, 1, :], bn[:, 2, :]))
            link(dve.scalar_tensor_tensor(bn[:, 2, :], bn[:, 1, :], 2.0, prm[:, L2_G:L2_G + 6], ALU.mult, ALU.mult))
            link(dve.tensor_tensor(bn[:, 3, :], prm[:, L2_M:L2_M + 6], bn[:, 2, :], ALU.mult))
            link(dve.tensor_tensor(bn[:, 3, :], prm[:, L2_B:L2_B + 6], bn[:, 3, :], ALU.subtract))
            dve.wait_ge(iota_done, 6)
            link, done = chain(bn_done, 5)
            link(dve.tensor_scalar(pix[:, 1:2], pix[:, 0:1], 5, None, ALU.arith_shift_right), False)
            link(dve.tensor_scalar(pix[:, 2:3], pix[:, 0:1], W - 1, None, ALU.bitwise_and))
            link(dve.tensor_copy(pixf[:], pix[:, 1:3]))
            for a in range(2):
                link(dve.tensor_scalar(grid[:, :, :, a], grid_i[:, :, :, a], pixf[:, a:a + 1], None, ALU.add), False)
            link(dve.tensor_scalar(band[:], cell_i[:, 0:W, 0], pixf[:, 1:2], None, ALU.subtract), False)
            link(dve.tensor_scalar(col_i[:], col_i[:], FOLD - 1, None, ALU.bitwise_and))
            link(dve.tensor_scalar(wide[:], band[:], float(-PADK), None, ALU.is_ge))
            link(dve.scalar_tensor_tensor(band[:], band[:], float(PADK), wide[:], ALU.is_le, ALU.mult), False)
            link(dve.tensor_scalar(pick[:], col_i[:], 0.0, None, ALU.is_equal), False)
            link(dve.memset(first_entry[:], float(ENTRY)))

            def positions(image, u):
                link, done = chain(a_step, A_STEPS * image)
                NT = TILES * TAPS
                dve.wait_ge(a_off, image + 1)
                dve.tensor_tensor(pos[:].rearrange("p (t k) a -> p t (k a)", k=TAPS),
                                  bank[4][:, 0:NT * 2].rearrange("p (t o) -> p t o", t=TILES),
                                  offb_t[:].unsqueeze(1).to_broadcast([P, TILES, 2 * TAPS]), ALU.add).then_inc(a_read, 1)
                dve.wait_ge(a_read, image + 1)
                link(dve.tensor_tensor(pos[:], pos[:], grid[:].rearrange("p t k a -> p (t k) a"), ALU.add))
                link(dve.tensor_scalar(cell[:], pos[:], 0.0, float(W - 2), ALU.max, ALU.min))
                link(dve.tensor_copy(cell_i[:], cell[:]))
                link(dve.tensor_copy(far[:], cell_i[:]))
                link(dve.tensor_tensor(hat[:, 0], far[:], cell[:], ALU.is_gt))
                link(dve.tensor_tensor(cell[:], far[:], hat[:, 0], ALU.subtract))
                link(dve.tensor_tensor(far[:], pos[:], cell[:], ALU.subtract))
                link(dve.tensor_scalar(hat[:, 0], far[:], -1.0, 1.0, ALU.mult, ALU.add), False)
                link(dve.tensor_scalar(hat[:, 1], far[:], -1.0, 2.0, ALU.mult, ALU.add))
                link(dve.scalar_tensor_tensor(hat[:, 0], far[:], 1.0, hat[:, 0], ALU.add, ALU.min), False)
                link(dve.tensor_tensor(hat[:, 1], far[:], hat[:, 1], ALU.min))
                link(dve.tensor_scalar(hat[:], hat[:], 0.0, None, ALU.max))
                wv = wgt_all[:, image]
                for dy in range(2):
                    for dx in range(2):
                        link(dve.tensor_tensor(wv[:, :, 2 * dy + dx], hat[:, dy, :, 0], hat[:, dx, :, 1], ALU.mult), False)
                link(dve.scalar_tensor_tensor(entry[:], cell[:, :, 0], float(W), cell[:, :, 1], ALU.mult, ALU.add))
                link(dve.tensor_scalar(idx_all[:, image], entry[:],
                                       first_entry[:], None, ALU.add))
                link(dve.tensor_scalar(first_entry[:], first_entry[:], float(TABLE), None, ALU.add))
                assert done[0] == A_STEPS

            with dve.Fori(0, N // 2) as j:
                for u in range(2):
                    positions(2 * j + u, u)

            def gram(g, c, ic):
                h = g // 2
                link, done = chain(corr_step, CORR_STEPS * ic + HALF_STEPS * h + 3 * (g % 2))
                ps = bank[c % C_BANKS][:].rearrange("p (t r b) -> p t r b", t=2, b=W)
                dve.wait_ge(c_done, NC * ic + c + 1)
                for q in range(RT):
                    rows = slice(W * q, W * (q + 1))
                    ins = dve.tensor_tensor(corr[rows, 2 * (g % 2):2 * (g % 2) + 2, :, :], ps[rows, :, q:q + KS, :],
                                            band[rows].unsqueeze(1).unsqueeze(1).to_broadcast([W, 2, KS, W]), ALU.mult)
                    if q < RT - 1:
                        link(ins, False)
                ins.then_inc(c_drained[c % C_BANKS], 1)

            def window(h, c, ic):
                link, done = chain(corr_step, CORR_STEPS * ic + HALF_STEPS * h + 6)
                for cc in (c - 1, c):
                    dve.wait_ge(c_drained[cc % C_BANKS], drains(ic, cc) + 1)
                dve.wait_ge(corr_step, CORR_STEPS * ic + HALF_STEPS * h + 6)
                link(dve.tensor_reduce(folded[:], corr[:].rearrange("p t y (g r) -> p (t y) r g", r=FOLD),
                                       AX.X, ALU.add))
                link(dve.tensor_tensor(picked[:], folded[:].unsqueeze(2).to_broadcast([P, HT * KS, KS, FOLD]),
                                       pick[:].unsqueeze(1).to_broadcast([P, HT * KS, KS, FOLD]), ALU.mult))
                gv = gs[:, h]
                link(dve.tensor_reduce(gv.rearrange("p t (y x) -> p (t y) x", x=KS), picked[:], AX.X, ALU.add))
                link(dve.tensor_tensor(gsq[:], gv, gv, ALU.mult))
                link(dve.tensor_reduce(nrm[:, h, 2, :], gsq[:], AX.X, ALU.add))
                dve.tensor_scalar(nrm[:, h, 0, :], nrm[:, h, 2, :], L1_EPS, None, ALU.add).then_inc(norm_asked, 1)

            def normalise(h, ic):
                link, done = chain(corr_step, CORR_STEPS * ic + HALF_STEPS * h + 11)
                total, root, tmp = (nrm[:, h, a, :] for a in range(3))
                dve.wait_ge(norm_asked, 2 * ic + h + 1)
                dve.wait_ge(norm_root, 2 * ic + h + 1)
                link(dve.reciprocal(tmp, root))
                link(dve.tensor_tensor(tmp, tmp, total, ALU.mult))
                link(dve.tensor_tensor(tmp, tmp, root, ALU.add))
                link(dve.reciprocal(root, tmp))
                dve.scalar_tensor_tensor(gs[:, h], root.unsqueeze(2).to_broadcast([P, HT, NB]), 2.0, gs[:, h],
                                         ALU.mult, ALU.mult).then_inc(gs_done, 1)

            def body(items, ib, ic):
                for it in items:
                    if it[0] == "blend":
                        _, u, pair = it
                        if (u, pair) == (0, 0):
                            wait_past(dve, blended, UNITS * BLEND * ib)
                            dve.tensor_copy(idx[:], idx_all[:, ib]).then_inc(taken, 1)
                            dve.tensor_copy(wgt[:], wgt_all[:, ib]).then_inc(taken, 1)
                            dve.wait_ge(taken, 2 * ib + 2)
                        h, k = u // TAPS, u % TAPS
                        if pair == 0:
                            wait_past(dve, turned, UNITS * ib + u - 1)
                        base = (UNITS * ib + u) * BLEND + 8 * pair
                        for tt in range(2):
                            n = HT * u + 2 * pair + tt
                            dve.wait_ge(gathered[n % SLOTS], 16 * (UNITS * HT // SLOTS * ib + n // SLOTS + 1))
                        for corner in range(4):
                            for tt in range(2):
                                t = 2 * pair + tt
                                w_ = wgt[:, (HT * h + t) * TAPS + k, corner:corner + 1]
                                g_ = patch[:, (HT * u + t) % SLOTS, corner, :]
                                o_ = samp[:, u % 2, t, :]
                                if corner == 0:
                                    ins = dve.tensor_scalar(o_, g_, w_, None, ALU.mult)
                                else:
                                    dve.wait_ge(blended, base + 2 * corner + tt - 1)
                                    ins = dve.scalar_tensor_tensor(o_, g_, w_, o_, ALU.mult, ALU.add)
                                ins.then_inc(blended, 1)
                    elif it[0] == "out0":
                        _, h, m = it
                        dve.wait_ge(out0_done, 2 * KC * ib + KC * h + m + 1)
                        dve.wait_ge(ld_res[m], 16 * (2 * ib + h + 1))
                        dve.scalar_tensor_tensor(res[:, m, :], bank[6 + h][:], prm[:, L0_S3 + m:L0_S3 + m + 1],
                                                 res[:, m, :], ALU.mult, ALU.add).then_inc(b_drained[h], 1)
                    elif it[0] == "step":
                        c = it[1]
                        s = C_STEPS[c]
                        if s[0] == "gram":
                            if s[1] == 2:
                                normalise(0, ic)
                            gram(s[1], c, ic)
                            if s[1] % 2:
                                window(s[1] // 2, c, ic)
                        elif s == ("corrT", 0):
                            normalise(1, ic)
                        elif s[0] == "expand":
                            _, layer, h, m = s
                            dve.wait_ge(c_done, NC * ic + c + 1)
                            v = xs[:, m, h * HALF:(h + 1) * HALF]
                            sc = bn[:, 2, 2 + m:3 + m] if layer == 2 else prm[:, L3_S3 + m:L3_S3 + m + 1]
                            dve.scalar_tensor_tensor(v, bank[c % C_BANKS][:], sc, v, ALU.mult, ALU.add)\
                               .then_inc(c_drained[c % C_BANKS], 1)

            body(B_ONLY, 0, 0)
            with dve.Fori(1, N) as i:
                body(SCHEDULE, i, i - 1)
            body(C_ONLY, N, N - 1)


def kernel(**inputs):
    import numpy as np
    import concourse.bacc as bacc
    from concourse import mybir
    from concourse.bass_utils import run_bass_kernel_spmd

    a = {k: np.asarray(v) for k, v in inputs.items()}

    def lay(w):
        return np.transpose(w.reshape(w.shape[0], w.shape[1], TAPS), (1, 2, 0))

    def chunks(w):
        return np.transpose(w.T.reshape(-1, P, w.shape[0]), (1, 0, 2))

    def cols(*names):
        return [a[n].reshape(-1, P).T for n in names]

    par = np.concatenate(
        cols("L0_conv_bn1_s", "L0_conv_bn1_b", "L0_conv_bn2_s", "L0_conv_bn2_b", "L0_conv_bn3_s", "L0_conv_bn3_b",
             "L1_conv_b")
        + cols(*[f"L2_conv_{v}{n}" for v in "gbmv" for n in (1, 2, 3)])
        + cols("L3_conv_scale1", "L3_conv_bias1", "L3_conv_scale2", "L3_conv_bias2", "L3_conv_scale3",
               "L3_conv_bias3"), axis=1)
    arrays = {
        "x": a["x"],
        "w1t": chunks(a["L0_conv_conv1_w"][:, :, 0, 0]),
        "offwt": lay(a["L0_conv_off_w"]),
        "offb": np.broadcast_to(a["L0_conv_off_b"], (P, 2 * TAPS)),
        "w2t": lay(a["L0_conv_conv2_w"]),
        "w3t": a["L0_conv_conv3_w"][:, :, 0, 0].T,
        "l1wt": chunks(a["L1_conv_W"][:, :C]),
        "l1gt": a["L1_conv_W"][:, C:].T,
        "l2w1t": chunks(a["L2_conv_w1"][:, :, 0, 0]),
        "l2w2t": lay(a["L2_conv_w2"]),
        "l2w3t": a["L2_conv_w3"][:, :, 0, 0].T,
        "l3w1t": chunks(a["L3_conv_w1"][:, :, 0, 0]),
        "l3w2t": lay(a["L3_conv_w2"]),
        "l3w3t": a["L3_conv_w3"][:, :, 0, 0].T,
        "par": par,
    }
    nc = bacc.Bacc("TRN2", target_bir_lowering=False, num_devices=1)
    given, args = {}, []
    for name, v in arrays.items():
        v = np.ascontiguousarray(v)
        given[f"in_{name}"] = v
        args.append(nc.dram_tensor(f"in_{name}", v.shape, mybir.dt.from_np(v.dtype), kind="ExternalInput").ap())
    out = nc.dram_tensor("out_y", (N, C, H, W), mybir.dt.float32, kind="ExternalOutput").ap()
    conv_seq_kernel(nc, *args, out)
    r = run_bass_kernel_spmd(nc, [given], core_ids=[0])
    return r.results[0]["out_y"]
```

```python
import concourse.bass as bass
from concourse import mybir
from contextlib import ExitStack

N, C, H, W = 4, 512, 32, 32
P = 128
HW = H * W
KC = C // P
HALF = HW // 2
TAPS = 9
TILES = HW // P
RT = P // W
HT = TILES // 2
HR = H // 2
KS = 5
PADK = KS // 2
NB = KS * KS
PART = 32
FOLD = 8
UNITS = 2 * TAPS
OFFS = 2 * TAPS
SLOTS = 8
RES = 3
RING = 3
BLEND = 3 * HT
L1_EPS = 1e-6
BN_EPS = 1e-5

L0_S1, L0_B1, L0_S2, L0_B2, L0_S3, L0_B3 = 0, 1, 2, 3, 4, 8
L1_B = 12
L2_G, L2_B, L2_M, L2_V = 16, 22, 28, 34
L3_S1, L3_B1, L3_S2, L3_B2, L3_S3, L3_B3 = 40, 41, 42, 43, 44, 48
NPAR = 52

C_STEPS = ([("gram", g) for g in range(4)] + [("corrT", 0)] + [("mix", 0, m) for m in range(KC)]
           + [("corrT", 1)] + [("mix", 1, m) for m in range(KC)])
C_STEPS += [("reduce", 2, 0), ("reduce", 2, 1), ("conv", 2, 0), ("expand", 2, 0, 0), ("expand", 2, 0, 1),
            ("conv", 2, 1), ("expand", 2, 0, 2), ("expand", 2, 0, 3), ("expand", 2, 1, 0), ("expand", 2, 1, 1),
            ("reduce", 3, 0), ("expand", 2, 1, 2), ("expand", 2, 1, 3), ("reduce", 3, 1), ("conv", 3, 0),
            ("conv", 3, 1)] + [("expand", 3, h, m) for h in range(2) for m in range(KC)]
NC = len(C_STEPS)
STEP_AT = {s: c for c, s in enumerate(C_STEPS)}
C_BANKS = 4
TAKES = list(C_STEPS)
for h, n in ((0, 2), (1, 2)):
    TAKES.remove(("corrT", h))
    TAKES.insert(TAKES.index(("mix", h, n)), ("corrT", h))
TAKE = [TAKES.index(s) for s in C_STEPS]
BANK = [n % C_BANKS for n in TAKE]
BANK_USES = [BANK.count(b) for b in range(C_BANKS)]
SPLIT_STEPS = [c for c, s in enumerate(C_STEPS) if s[0] not in ("gram", "corrT") and s[:2] != ("expand", 3)]
RING_USE = {c: n for n, c in enumerate(c for c, s in enumerate(C_STEPS) if s[0] not in ("gram", "corrT"))}
A_PARTS = ("conv", "conv", "turn", "turn", "taps", "shift")


FIRST_BLEND = [("weigh", 0, 0), ("weigh", 0, 1), ("blend", 0, 0), ("blend", 0, 1)]
FIRST = [c for c, s in enumerate(C_STEPS) if s[0] == "conv" or s in [("mix", h, m) for h in range(2) for m in range(3)]]


def expands(layer, h, first):
    return [("expand", layer, h, m) for m in (first, first + 1)]


ROWS = [([("gram", 0), ("gram", 1), ("window", 0), ("root", 0), ("normalise", 0), ("blend", 0, 0), ("gram", 2),
          ("gram", 3), ("first", "mix", 0, 0), ("first", "mix", 0, 1), ("corrT", 0), ("first", "mix", 0, 2),
          ("blend", 0, 1)], [], []),
        ([("mix", 0, 0), ("mix", 0, 1), ("mix", 0, 2)], [0], []),
        ([("window", 1)], [], []),
        ([("mix", 0, 3), ("first", "mix", 1, 0)], [1], []), ([("root", 1), ("normalise", 1)], [], []),
        ([("first", "mix", 1, 1)], [2], []),
        ([("corrT", 1), ("first", "mix", 1, 2)], [], []), ([("mix", 1, 0)], [3], [])]
ROWS += [([("mix", 1, m)], [3 + m], []) for m in range(1, KC)]
ROWS += [([("reduce", 2, 0)], [7], []), ([("reduce", 2, 1)], [8], []), ([("first", "conv", 2, 0)], [9], []),
         ([("conv", 2, 0)], [10], []), ([("hidlow", 0), ("first", "conv", 2, 1)], [11], []),
         (expands(2, 0, 0), [], [(0, 0)]), ([("conv", 2, 1)], [12], []), (expands(2, 0, 2), [], []),
         (expands(2, 1, 0), [13], []), ([("reduce", 3, 0)], [14], []), (expands(2, 1, 2), [], []), ([], [15], [(0, 1)]),
         ([("reduce", 3, 1)], [], []), ([("first", "conv", 3, 0)], [16], [(0, 2)]), ([("conv", 3, 0)], [17], [(0, 3)]),
         ([("first", "conv", 3, 1)], [], []), ([("hidlow", 1), ("conv", 3, 1)], [], [(1, 0)]),
         (expands(3, 0, 0), [], [(1, 1)]), (expands(3, 0, 2), [], [(1, 2)]), (expands(3, 1, 0), [], [(1, 3)]),
         (expands(3, 1, 2), [], [])]


def row_items(middle, units, outs, pending):
    items = []
    steps = [it[1] for it in middle if it[0] == "step"]
    for n, u in enumerate(units or [None]):
        if u is not None and u + 1 < UNITS:
            items += [("weigh", u + 1, 0), ("weigh", u + 1, 1), ("blend", u + 1, 0), ("blend", u + 1, 1)]
        items += [("outhigh", *it[1:]) for it in pending if it[0] == "outlow"]
        late = [it for it in pending if it[0] == "outlow"]
        if n == 0:
            items += middle
        items += [it for it in pending if it[0] == "tap"]
        pending.clear()
        if u is not None:
            items.append(("turn", u))
        if n == 0 and steps and steps[-1] in SPLIT_STEPS:
            items.append(("fine", steps[-1]))
        if u is not None:
            items.append(("low", u))
        if middle:
            items += late
            late = []
        if u is not None:
            if u:
                items.append(("tap", u - 1))
            if u == UNITS - 1:
                pending.append(("tap", u))
    for h, m in outs:
        items += [("out0", h, m)] + late
        late = []
        pending.append(("outlow", h, m))
    return items + late


def build_schedule():
    items, pending, order = [("take",)], [], []
    for steps, units, outs in ROWS:
        middle, last = [], None
        for s in steps:
            if s == ("blend", 0, 0):
                middle += FIRST_BLEND[:3]
            elif s[0] == "first":
                middle.append(("first", STEP_AT[s[1:]]))
            elif s in STEP_AT:
                order.append(s)
                middle.append(("step", STEP_AT[s]))
                if last in SPLIT_STEPS:
                    middle.append(("fine", last))
                last = STEP_AT[s]
            else:
                middle.append(s)
        items += row_items(middle, units, outs, pending)
    assert order == C_STEPS
    assert not pending
    return items


def build_prologue():
    items = [("a", 0, k) for k in range(len(A_PARTS))] + [("positions", 0), ("take",)] + FIRST_BLEND
    rows, pending = [], []
    for i in range(1, N):
        rows += [[("a", i, 0)], [("positions", i - 1)] * (i > 1) + [("a", i, 1), ("a", i, 2)],
                 [("a", i, 3), ("a", i, 4)], [("a", i, 5)]]
    rows += [[("positions", N - 1), ("scale", 0), ("scale", 1)], [("split", 0), ("split", 1)],
             [("split low", 0), ("split low", 1), ("split", 2), ("split", 3)],
             [("split low", 2), ("split low", 3), ("split", 4), ("split", 5)],
             [("split low", 4), ("split", 6), ("split corr",)]]
    for u in range(UNITS):
        middle = rows.pop(0) if rows else []
        if u == TAPS + 1:
            middle = middle + [("hidlow", 0)]
        outs = [(0, u - TAPS - 2)] if u in range(TAPS + 2, TAPS + 2 + KC) else []
        items += row_items(middle, [u], outs, pending)
    items += row_items([], [], [], pending) + [("split low", 5), ("split low", 6), ("hidlow", 1)]
    for m in range(KC):
        items += row_items([], [], [(1, m)], pending) + [("split low", 7)] * (m == 0)
    return items + row_items([], [], [], pending)


SCHEDULE = build_schedule()
PROLOGUE = build_prologue()
EPILOGUE = [it for it in SCHEDULE if it[0] in ("step", "fine", "first", "window", "root", "normalise")]
FINE_AT = {it[1]: n for n, it in enumerate(it for it in SCHEDULE if it[0] == "fine")}
FINES = len(FINE_AT)
assert sorted(FINE_AT) == SPLIT_STEPS


def drains(ic, c):
    return ic * BANK_USES[BANK[c]] + TAKE[c] // C_BANKS + 1


def fined(ic, c):
    return FINES * ic + FINE_AT[c] + 2


def slot_stores(slot):
    return [c for c in RING_USE if C_STEPS[c][:2] == ("expand", 3) and RING_USE[c] % RING == slot]


def wait_past(eng, sem, value):
    if not (isinstance(value, int) and value <= 0):
        eng.wait_ge(sem, value)


def conv_seq_kernel(nc, x, w1t, offwt, offb, w2t, w3t, l1wt, l1gt, l2w1t, l2w2t, l2w3, l3w1t, l3w2t, l3w3,
                    par, out):
    fp32 = mybir.dt.float32
    fp32r = mybir.dt.float32r
    i32 = mybir.dt.int32
    ALU = mybir.AluOpType
    ACT = mybir.ActivationFunctionType
    AX = mybir.AxisListType

    x_v = x.rearrange("n (k p) a b -> n p k (a b)", p=P)
    out_v = out.rearrange("n (k p) a b -> n k p (a b)", p=P)
    table_0 = nc.dram_tensor("patch_table_0", (HW, 2 * P), fp32, kind="Internal")
    table_n = nc.dram_tensor("patch_tables", ((N - 1) * HW, 2 * P), fp32, kind="Internal")
    patches_0, patches_n = table_0.ap()[0:HW - W], table_n.ap()[0:(N - 1) * HW - W]

    ctx = ExitStack()
    with ctx:
        def sb(name, shape, dt=fp32, stack=ctx):
            return stack.enter_context(nc.sbuf_tensor(name, shape, dt))

        def two(name, shape, stack=ctx):
            return [sb(f"{name}_{part}", shape, fp32r, stack) for part in ("high", "low")]

        def sem(name):
            return ctx.enter_context(nc.semaphore(name))

        w2 = two("w2", [P, TAPS, P])
        w3 = two("w3", [P, C])
        l1g = sb("l1g", [3 * PART, C], fp32r)
        gs = sb("gs", [P, HT, 3, PART])
        wr = {n: two(f"l{n}w1", [P, KC, P]) for n in (2, 3)}
        wc = {n: two(f"l{n}w2", [P, TAPS, P]) for n in (2, 3)}
        we = {n: two(f"l{n}w3", [P, C]) for n in (2, 3)}
        prm = sb("prm", [P, NPAR])
        bn = sb("bn", [P, 4, 6])
        ident_r = sb("ident_r", [P, P], fp32r)
        ident = ident_r[:].bitcast(fp32)
        band = sb("band", [P, W])
        pick = sb("pick", [P, KS, FOLD])
        idx_all = sb("idx_all", [P, N, TILES * TAPS], i32)
        wgt_all = sb("wgt_all", [P, N, TILES * TAPS, 4])
        tick = sb("tick", [1, 1 + 2 * UNITS])
        idx = sb("idx", [P, TILES * TAPS], i32)
        wgt = sb("wgt", [P, TILES * TAPS, 4])
        patch = sb("patch", [P, SLOTS, 4, P])
        samp = sb("samp", [P, 2, HT, P])
        sampT = two("sampT", [P, 2, HALF])
        hid = two("hid", [P, HALF])
        hidf = sb("hidf", [P, HALF])
        res = sb("res", [P, RES, HALF])
        ring = sb("ring", [P, RING, HALF])
        x1 = two("x1", [P, KC, H + 2 * PADK, W])

        with ExitStack() as early:
            xa = [sb(f"xa{u}", [P, KC, HW], stack=early) for u in range(2)]
            w1 = sb("w1", [P, KC, P], stack=early)
            ident_f = sb("ident_f", [P, P], stack=early)
            wide = sb("wide", [P, W], stack=early)
            offw = sb("offw", [P, TAPS * OFFS], stack=early)
            offb_t = sb("offb_t", [P, OFFS], stack=early)
            mid = sb("mid", [P, HW], stack=early)
            midT = [sb(f"midT{u}", [P, TILES, P], stack=early) for u in range(2)]
            tapped = sb("tapped", [P, TILES, TAPS, OFFS], stack=early)
            dist = sb("dist", [P, P], i32, stack=early)
            shifts = sb("shifts", [P, 3, 5, P], stack=early)
            grid_i = sb("grid_i", [P, TILES, TAPS, 2], i32, stack=early)
            grid = sb("grid", [P, TILES, TAPS, 2], stack=early)
            pix = sb("pix", [P, 4], i32, stack=early)
            pixf = sb("pixf", [P, 2], stack=early)
            col_i = sb("col_i", [P, KS, FOLD], i32, stack=early)
            pos = sb("pos", [P, TILES * TAPS, 2], stack=early)
            cell = sb("cell", [P, TILES * TAPS, 2], stack=early)
            cell_i = sb("cell_i", [P, TILES * TAPS, 2], i32, stack=early)
            far = sb("far", [P, TILES * TAPS, 2], stack=early)
            hat = sb("hat", [P, 2, TILES * TAPS, 2], stack=early)
            entry = sb("entry", [P, TILES * TAPS], stack=early)
        xs = two("xs", [P, KC, HW])
        hp = two("hp", [P, H + 2, W + 2])
        with ExitStack() as layer1:
            corr = sb("corr", [P, HT, KS, W], stack=layer1)
            folded = sb("folded", [P, HT * KS, FOLD], stack=layer1)
            picked = sb("picked", [P, HT * KS, KS, FOLD], stack=layer1)
            gsT = sb("gsT", [3 * PART, HALF], fp32r, stack=layer1)
        h2 = two("h2", [P, 2, HALF])
        raw = sb("raw", [P, 2, HT, NB])
        gsq = sb("gsq", [P, HT, NB])
        nrm = sb("nrm", [P, 2, 3, HT])
        l1w = two("l1w", [P, KC, C])

        bank = [ctx.enter_context(nc.psum_tensor(f"bank{b}", [P, HALF], fp32)) for b in range(8)]

        st0 = xa[0][:].rearrange("p k s -> p (k s)")
        st1 = xa[1][:].rearrange("p k s -> p (k s)")
        SPLITS = [(st0[:, 4 * C:5 * C], we[2], l2w3, 0), (st0[:, 5 * C:6 * C], we[3], l3w3, 0),
                  (st0[:, 0:4 * C], l1w, l1wt, 0),
                  (st1[:, 0:C], wr[2], l2w1t, 1), (st1[:, C:C + TAPS * P], wc[2], l2w2t, 1),
                  (st1[:, C + TAPS * P:2 * C + TAPS * P], wr[3], l3w1t, 1),
                  (st1[:, 2 * C + TAPS * P:2 * C + 2 * TAPS * P], wc[3], l3w2t, 1)]
        corr_stage = st1[:, 2 * C + 2 * TAPS * P:3 * C + 2 * TAPS * P]
        pt = patch[:].rearrange("p s a c -> p (s a c)")
        FIRST_SPLITS = [(pt[:, 0:TAPS * P], w2, w2t), (pt[:, TAPS * P:TAPS * P + C], w3, w3t)]

        def flat(t):
            return t[:].rearrange("p a b -> p (a b)") if len(t.shape) == 3 else t[:]

        ld_first, ld_deform = sem("ld_first"), sem("ld_deform")
        ld_late = [sem(f"ld_late{u}") for u in range(2)]
        ld_corr = sem("ld_corr")
        ld_xa = [sem(f"ld_xa{n}") for n in range(4)]
        iota_done, const_done, borders_done = sem("iota_done"), sem("const_done"), sem("borders_done")
        root_asked, root_done, bn_done = sem("root_asked"), sem("root_done"), sem("bn_done")
        a_done, a_drained, a_step, a_read = sem("a_done"), sem("a_drained"), sem("a_step"), sem("a_read")
        high_done, low_done = sem("high_done"), sem("low_done")
        tabled = [sem(f"tabled{u}") for u in range(2)]
        taken, ticked = sem("taken"), sem("ticked")
        gathered = [sem(f"gathered{s}") for s in range(SLOTS)]
        blended = sem("blended")
        turned, sampT_high, sampT_low, tap_done = (sem(n) for n in ("turned", "sampT_high", "sampT_low", "tap_done"))
        hid_read, hid_high, hid_low = sem("hid_read"), sem("hid_high"), sem("hid_low")
        out0_done, res_summed, res_relu, x1_high, x1_low = (
            sem(n) for n in ("out0_done", "res_summed", "res_relu", "x1_high", "x1_low"))
        ld_res = [sem(f"ld_res{n}") for n in range(RES)]
        c_done = sem("c_done")
        c_drained = [sem(f"c_drained{b}") for b in range(C_BANKS)]
        corr_step, norm_asked, norm_root, gs_done = (
            sem(n) for n in ("corr_step", "norm_asked", "norm_root", "gs_done"))
        step_high, fine_done = sem("step_high"), sem("fine_done")
        stored = [sem(f"stored{n}") for n in range(RING)]
        weighed = sem("weighed")
        gsT_high, corr_high, corr_low = sem("gsT_high"), sem("corr_high"), sem("corr_low")
        scaled, scaled_turned, ident_done = sem("scaled"), sem("scaled_turned"), sem("ident_done")

        block = ctx.enter_context(nc.Block())

        CONSTS = 27
        A_STEPS = 18
        HALF_STEPS = 15
        CORR_STEPS = 30
        FIRST_TAPS = 6
        HIGH_AT = {c: n for n, c in enumerate(SPLIT_STEPS)}

        def out_bank(h, m):
            return 6 + (h + m) % 2 if h else 6

        def slot(c):
            return ring[:, RING_USE[c] % RING, :]

        def table_dmas(parity, images):
            return 16 * sum(5 if i < 2 else 4 for i in range(parity, images, 2))

        def slot_free(eng, ic, c):
            n = RING_USE[c] - RING
            before = [x for x in RING_USE if RING_USE[x] == n]
            mine = slot_stores(n % RING)
            if n < 0:
                eng.wait_ge(stored[n % RING], 16 * len(mine) * ic + 1)
            elif before[0] in SPLIT_STEPS:
                eng.wait_ge(fine_done, fined(ic, before[0]))
            else:
                eng.wait_ge(stored[n % RING], 16 * (len(mine) * ic + mine.index(before[0]) + 1) + 1)

        def split_parts(c):
            s = C_STEPS[c]
            if s[0] in ("mix", "expand"):
                h, m = s[-2:]
                return slot(c), *(xs[p][:, m, h * HALF:(h + 1) * HALF] for p in range(2))
            if s[0] == "reduce":
                rows = slice(1 + HR * s[2], 1 + HR * (s[2] + 1))
                return slot(c).rearrange("p (a b) -> p a b", b=W), *(hp[p][:, rows, 1:W + 1] for p in range(2))
            return slot(c), *(h2[p][:, s[2], :] for p in range(2))

        @block.sync
        def _(sp):
            def load_x(i, h):
                sp.dma_start(xa[i % 2][:, :, h * HALF:(h + 1) * HALF],
                             x_v[i, :, :, h * HALF:(h + 1) * HALF]).then_inc(ld_xa[2 * (i % 2) + h], 16)

            sp.dma_start(w1[:], w1t).then_inc(ld_first, 16)
            load_x(0, 0)
            load_x(0, 1)
            for t, d in ((prm, par), (offw, offwt), (offb_t, offb)):
                sp.dma_start(t[:], d).then_inc(ld_first, 16)
            for stage, _, d in FIRST_SPLITS:
                sp.dma_start(stage, d).then_inc(ld_deform, 16)
            load_x(1, 0)
            load_x(1, 1)
            def load_res(n, ib):
                h, m = n // KC, n % KC
                if n == 0:
                    wait_past(sp, x1_low, 8 * ib)
                elif n >= RES:
                    sp.wait_ge(x1_low, 8 * ib + n - RES + 1)
                sp.dma_start(res[:, n % RES, :], x_v[ib, :, m, h * HALF:(h + 1) * HALF]).then_inc(ld_res[n % RES], 16)

            def body(items, ib, ic):
                if ib is not None:
                    for n in range(RES):
                        load_res(n, ib)
                for it in items:
                    if it[0] == "a":
                        _, i, k = it
                        if k in (1, 3) and 1 <= i < N - 1:
                            sp.wait_ge(a_done, 8 * (i - 1) + 2)
                            load_x(i + 1, k // 2)
                        if k == 3 and i >= N - 2:
                            sp.wait_ge(a_done, 8 * i + 2)
                            for stage, _, d, u in SPLITS:
                                if u == i % 2:
                                    sp.dma_start(stage, d if len(d.shape) == 2 else d.rearrange("p a b -> p (a b)"))\
                                      .then_inc(ld_late[u], 16)
                            if i == N - 1:
                                for p in range(3):
                                    sp.dma_start(corr_stage[PART * p:PART * p + NB], l1gt).then_inc(ld_corr, 16)
                        if A_PARTS[k] == "turn":
                            h = k - 2
                            sp.wait_ge(a_drained, 7 * i + 3 + h)
                            table = (table_n if i else table_0).ap()
                            turned_ = midT[i % 2]
                            done = tabled[i % 2]
                            for above in range(2):
                                first = HW * max(i - 1, 0) + HALF * h - above * W
                                cols = slice(above * P, (above + 1) * P)
                                tiles = HT
                                if first < 0:
                                    sp.dma_start(table[0:P - W, cols], turned_[W:P, 0, :]).then_inc(done, 16)
                                    first, tiles = P - W, HT - 1
                                sp.dma_start(table[first:first + tiles * P, cols].rearrange("(t p) c -> p t c", p=P),
                                             turned_[:, HT * h + HT - tiles:HT * h + HT, :]).then_inc(done, 16)
                    if it[0] == "outlow" and KC * it[1] + it[2] + RES < 2 * KC:
                        load_res(KC * it[1] + it[2] + RES, ib)
                    if it[0] == "step" and C_STEPS[it[1]][:2] == ("expand", 3):
                        _, _, h, m = C_STEPS[it[1]]
                        c = it[1]
                        sp.wait_ge(c_drained[BANK[c]], drains(ic, c) + 1)
                        sp.dma_start(out_v[ic, m, :, h * HALF:(h + 1) * HALF], slot(c))\
                          .then_inc(stored[RING_USE[c] % RING], 16)

            body(PROLOGUE, 0, None)
            for n in range(RING):
                sp.sem_inc(stored[n], 1)
            with sp.Fori(1, N) as i:
                body(SCHEDULE, i, i - 1)
            body(EPILOGUE, None, N - 1)
            for n in range(RING):
                sp.wait_ge(stored[n], 16 * len(slot_stores(n)) * N + 1)

        @block.gpsimd
        def _(pool):
            pool.iota(pix[:, 0:1], [[0, 1]], base=0, channel_multiplier=1).then_inc(iota_done, 1)
            pool.iota(dist[:], [[-1, P]], base=0, channel_multiplier=1).then_inc(iota_done, 1)
            pool.iota(grid_i[:, :, :, 0].rearrange("p t (a b) -> p t a b", b=3), [[RT, TILES], [1, 3], [0, 3]],
                      base=-1, channel_multiplier=0).then_inc(iota_done, 1)
            pool.iota(grid_i[:, :, :, 1].rearrange("p t (a b) -> p t a b", b=3), [[0, TILES], [0, 3], [1, 3]],
                      base=-1, channel_multiplier=0).then_inc(iota_done, 1)
            pool.iota(col_i[:, :, :], [[1, KS], [-1, FOLD]], base=2 * FOLD - PADK, channel_multiplier=1)\
                .then_inc(iota_done, 1)
            pool.iota(cell_i[:, 0:W, 0], [[1, W]], base=0, channel_multiplier=0).then_inc(iota_done, 1)
            pool.memset(ident_f[:], 0.0).then_inc(iota_done, 1)
            pool.wait_ge(iota_done, 7)
            pool.affine_select(out=ident_f[:], in_=ident_f[:], compare_op=ALU.not_equal, fill=1.0, base=0,
                               pattern=[[-1, P]], channel_multiplier=1).then_inc(const_done, 1)
            pool.memset(tick[:], 0.0).then_inc(borders_done, 1)
            pool.memset(l1g[:].bitcast(fp32), 0.0).then_inc(borders_done, 1)
            pool.memset(gs[:], 0.0).then_inc(borders_done, 1)
            for part in range(2):
                pool.memset(x1[part][:, :, 0:PADK, :].bitcast(fp32), 0.0).then_inc(borders_done, 1)
                pool.memset(x1[part][:, :, H + PADK:, :].bitcast(fp32), 0.0).then_inc(borders_done, 1)
            pool.wait_ge(borders_done, 7)
            pool.wait_ge(tabled[0], table_dmas(0, 1))
            pool.wait_ge(low_done, 2)

            def freed_by(n):
                u, t = n // HT, n % HT
                return u * BLEND + 6 * (t // 2) + 6

            def gather(u, ib):
                table = patches_0 if isinstance(ib, int) else patches_n
                h, k = u // TAPS, u % TAPS
                for t in range(HT):
                    n = HT * u + t
                    if t % 2 == 0:
                        wait_past(pool, blended, UNITS * BLEND * ib + freed_by(n - SLOTS))
                        p = 1 + 2 * u + t // 2
                        pool.tensor_tensor(tick[:, p:p + 1], tick[:, 0:1], tick[:, 0:1], ALU.add).then_inc(ticked, 1)
                    e = (HT * h + t) * TAPS + k
                    pool.indirect_dma_start(patch[:, n % SLOTS].rearrange("p a c -> p (a c)"), None, table,
                                            bass.IndirectOffsetOnAxis(ap=idx[:, e:e + 1], axis=0))\
                        .then_inc(gathered[n % SLOTS], 16)

            def body(items, ib, ic):
                for it in items:
                    if it[0] == "take":
                        wait_past(pool, ticked, 2 * UNITS * ib)
                        pool.wait_ge(taken, 2 * ib + 2)
                        gather(0, ib)
                    if it[0] == "blend" and it[1] + 1 < UNITS and it[2] == 0:
                        gather(it[1] + 1, ib)

            body(PROLOGUE, 0, None)
            pool.wait_ge(a_done, 8 * N)
            pool.wait_ge(a_drained, 7 * N)
            pool.wait_ge(a_step, A_STEPS * N)
            pool.wait_ge(tabled[0], table_dmas(0, N))
            pool.wait_ge(tabled[1], table_dmas(1, N))
            pool.wait_ge(low_done, 9)
            for part in range(2):
                pool.memset(hp[part][:].bitcast(fp32), 0.0).then_inc(borders_done, 1)
            with pool.Fori(1, N) as i:
                body(SCHEDULE, i, i - 1)

        @block.tensor
        def _(pe):
            def product(ps, w, a, start, stop):
                pe.matmul(ps, w[0], a[0], start=start, stop=False)
                pe.matmul(ps, w[0], a[1], start=False, stop=False)
                return pe.matmul(ps, w[1], a[0], start=False, stop=stop)

            pe.wait_ge(ld_first, 64)
            pe.wait_ge(ident_done, 1)

            def part_a(i, k):
                if A_PARTS[k] == "conv":
                    h = k
                    pe.wait_ge(ld_xa[2 * (i % 2) + h], 16 * (i // 2 + 1))
                    wait_past(pe, a_drained, 7 * (i - 1) + 5 + h)
                    for c in range(KC):
                        last = pe.matmul(bank[h][:], w1[:, c, :], xa[i % 2][:, c, h * HALF:(h + 1) * HALF],
                                         start=c == 0, stop=c == KC - 1)
                    last.then_inc(a_done, 1)
                elif A_PARTS[k] == "turn":
                    h = k - 2
                    pe.wait_ge(a_drained, 7 * i + h + 1)
                    wait_past(pe, a_drained, 7 * i)
                    wait_past(pe, a_read, i)
                    for t in range(HT):
                        last = pe.transpose(bank[2 + h][:, t * P:(t + 1) * P],
                                            mid[:, (HT * h + t) * P:(HT * h + t + 1) * P], ident)
                    last.then_inc(a_done, 1)
                elif A_PARTS[k] == "taps":
                    for g in range(3):
                        tiles = range(3 * g, min(3 * g + 3, TILES))
                        pe.wait_ge(a_drained, 7 * i + (2, 2, 3)[g])
                        for t in tiles:
                            last = pe.matmul(bank[g][:, (t - 3 * g) * TAPS * OFFS:(t - 3 * g + 1) * TAPS * OFFS],
                                             mid[:, t * P:(t + 1) * P], offw[:], start=True, stop=True)
                        last.then_inc(a_done, 1)
                else:
                    pe.wait_ge(a_drained, 7 * i + 7)
                    pe.wait_ge(low_done, 2)
                    pe.wait_ge(bn_done, 5 + CONSTS)
                    ps = bank[3][:, 0:TILES * OFFS]
                    for tap in range(TAPS):
                        pe.matmul(ps, shifts[:, tap % 3, tap // 3, :], tapped[:, :, tap, :],
                                  start=tap == 0, stop=False)
                    for row, r in ((0, 3), (2, 4)):
                        n = (TILES - 1) * OFFS
                        to, frm = (OFFS, 0) if row == 0 else (0, 1)
                        for col in range(3):
                            last = pe.matmul(ps[:, to:to + n], shifts[:, col, r, :],
                                             tapped[:, frm:frm + TILES - 1, 3 * row + col, :],
                                             start=False, stop=(row, col) == (2, 2))
                    last.then_inc(a_done, 1)

            def first(c, ic):
                s = C_STEPS[c]
                ps = bank[BANK[c]]
                pe.wait_ge(c_drained[BANK[c]], drains(ic, c))
                if s[0] == "mix":
                    _, h, m = s
                    for k in range(KC):
                        product(ps[:], [l1w[p][:, k, m * P:(m + 1) * P] for p in range(2)],
                                [x1[p][:, k, PADK + HR * h:PADK + HR * (h + 1), :] for p in range(2)], k == 0, False)
                else:
                    pe.wait_ge(fine_done, fined(ic, STEP_AT[("reduce", s[1], s[2])]))
                    conv_taps(c, range(FIRST_TAPS))

            def conv_taps(c, taps):
                _, layer, h = C_STEPS[c]
                for k in taps:
                    row, col = HR * h + k // 3, k % 3
                    last = product(bank[BANK[c]][:], [wc[layer][p][:, k, :] for p in range(2)],
                                   [hp[p][:, row:row + HR, col:col + W] for p in range(2)], k == 0, k == TAPS - 1)
                return last

            def step(c, ic):
                s = C_STEPS[c]
                ps = bank[BANK[c]]
                if s[0] == "mix" and c not in FIRST:
                    first(c, ic)
                elif c not in FIRST:
                    pe.wait_ge(c_drained[BANK[c]], drains(ic, c))
                if s[0] == "gram":
                    if s[1] < 2:
                        pe.wait_ge(x1_low, 8 * ic + KC * (s[1] + 1))
                    for half in range(2):
                        t = 2 * s[1] + half
                        for k in range(KC):
                            own = [x1[p][:, k, RT * t + PADK:RT * t + PADK + RT, :] for p in range(2)]
                            near = [x1[p][:, k, RT * t:RT * t + 2 * RT, :] for p in range(2)]
                            last = product(ps[:, half * 2 * P:(half + 1) * 2 * P], own, near, k == 0, k == KC - 1)
                elif s[0] == "corrT":
                    h = s[1]
                    pe.wait_ge(gs_done, 6 * ic + 3 * h + 3)
                    for t in range(HT):
                        last = pe.transpose(ps[0:3 * PART, t * P:(t + 1) * P],
                                            gs[:, t].rearrange("p a b -> p (a b)"), ident)
                elif s[0] == "mix":
                    _, h, m = s
                    ct = STEP_AT[("corrT", h)]
                    pe.wait_ge(c_drained[BANK[ct]], drains(ic, ct) + 1)
                    last = pe.matmul(ps[:], l1g[:, m * P:(m + 1) * P], gsT[:], start=False, stop=True)
                elif s[0] == "reduce":
                    _, layer, h = s
                    source = [STEP_AT[("mix", h, m) if layer == 2 else ("expand", 2, h, m)] for m in range(KC)]
                    pe.wait_ge(fine_done, fined(ic, max(source, key=FINE_AT.get)))
                    for k in range(KC):
                        last = product(ps[:], [wr[layer][p][:, k, :] for p in range(2)],
                                       [xs[p][:, k, h * HALF:(h + 1) * HALF] for p in range(2)], k == 0, k == KC - 1)
                elif s[0] == "conv":
                    _, layer, h = s
                    pe.wait_ge(fine_done, fined(ic, STEP_AT[("reduce", layer, 1)]))
                    last = conv_taps(c, range(FIRST_TAPS, TAPS))
                elif s[0] == "expand":
                    _, layer, h, m = s
                    pe.wait_ge(fine_done, fined(ic, STEP_AT[("conv", layer, h)]))
                    for p in range(2):
                        pe.matmul(ps[:], ident_r[:], xs[p][:, m, h * HALF:(h + 1) * HALF], start=p == 0, stop=False)
                    last = product(ps[:], [we[layer][p][:, m * P:(m + 1) * P] for p in range(2)],
                                   [h2[p][:, h, :] for p in range(2)], False, True)
                last.then_inc(c_done, 1)

            def body(items, ib, ic):
                for it in items:
                    if it[0] == "a":
                        part_a(it[1], it[2])
                    elif it[0] == "split" and it[1] < 2:
                        pe.wait_ge(scaled, KC * (it[1] + 1))
                        pe.wait_ge(a_drained, 7 * N)
                        pe.wait_ge(a_read, N)
                        for m in range(KC):
                            last = pe.transpose(bank[it[1]][:, m * P:(m + 1) * P],
                                                SPLITS[it[1]][0][:, m * P:(m + 1) * P], ident)
                        last.then_inc(scaled_turned, 1)
                    elif it[0] == "first":
                        first(it[1], ic)
                    elif it[0] == "step":
                        step(it[1], ic)
                    elif it[0] == "turn":
                        u = it[1]
                        pe.wait_ge(blended, (UNITS * ib + u + 1) * BLEND)
                        wait_past(pe, sampT_low, UNITS * ib + u - 1)
                        for t in range(HT):
                            last = pe.transpose(bank[4 + u % 2][:, t * P:(t + 1) * P], samp[:, u % 2, t, :], ident)
                        last.then_inc(turned, 1)
                    elif it[0] == "tap":
                        u = it[1]
                        h, k = u // TAPS, u % TAPS
                        if k == 0:
                            wait_past(pe, res_summed, 8 * ib)
                        pe.wait_ge(sampT_low, UNITS * ib + u + 1)
                        product(bank[6 + h][:], [w2[p][:, k, :] for p in range(2)],
                                [sampT[p][:, u % 2, :] for p in range(2)], k == 0, k == TAPS - 1).then_inc(tap_done, 1)
                    elif it[0] == "out0":
                        _, h, m = it
                        pe.wait_ge(hid_low, 2 * ib + h + 1)
                        b = out_bank(h, m)
                        if h == 1 and m == 1:
                            pe.wait_ge(res_summed, 8 * ib + KC)
                        elif m:
                            pe.wait_ge(res_summed, 8 * ib + KC * h + m - h)
                        product(bank[b][:], [w3[p][:, m * P:(m + 1) * P] for p in range(2)],
                                [hid[p][:] for p in range(2)], True, True).then_inc(out0_done, 1)

            body(PROLOGUE, 0, None)
            pe.wait_ge(corr_low, 1)
            pe.wait_ge(borders_done, 9)
            pe.wait_ge(ident_done, 1)
            pe.wait_ge(low_done, 9)
            with pe.Fori(1, N) as i:
                body(SCHEDULE, i, i - 1)
            body(EPILOGUE, None, N - 1)

        @block.scalar
        def _(act):
            def col(n):
                return prm[:, n:n + 1]

            act.wait_ge(const_done, 1)
            act.activation(ident_r[:], ident_f[:], ACT.Copy).then_inc(ident_done, 1)
            act.wait_ge(ld_first, 64)
            act.wait_ge(root_asked, 1)
            act.activation(bn[:, 0, :], bn[:, 1, :], ACT.Sqrt).then_inc(root_done, 1)

            def part_a(i, k):
                if A_PARTS[k] == "conv":
                    act.wait_ge(a_done, 8 * i + k + 1)
                    act.activation(mid[:, k * HALF:(k + 1) * HALF], bank[k][:], ACT.Relu,
                                   bias=col(L0_B1), scale=col(L0_S1)).then_inc(a_drained, 1)
                elif A_PARTS[k] == "turn":
                    h = k - 2
                    act.wait_ge(a_done, 8 * i + k + 1)
                    wait_past(act, tabled[i % 2], table_dmas(i % 2, i))
                    act.activation(midT[i % 2][:, HT * h:HT * (h + 1), :],
                                   bank[2 + h][:].rearrange("p (t c) -> p t c", c=P), ACT.Copy).then_inc(a_drained, 1)
                elif A_PARTS[k] == "taps":
                    wait_past(act, a_done, 8 * i)
                    for g in range(3):
                        n = min(3, TILES - 3 * g)
                        act.wait_ge(a_done, 8 * i + 5 + g)
                        act.activation(tapped[:, 3 * g:3 * g + n].rearrange("p t k o -> p (t k o)"),
                                       bank[g][:, 0:n * TAPS * OFFS], ACT.Copy).then_inc(a_drained, 1)

            def split(n):
                stage, w, _, u = SPLITS[n]
                act.wait_ge(ld_late[u], 16 * len([s for s in SPLITS if s[3] == u]))
                if w is l1w:
                    act.wait_ge(a_step, A_STEPS * N)
                    act.wait_ge(tabled[0], table_dmas(0, N))
                    act.wait_ge(tabled[1], table_dmas(1, N))
                if n < 2:
                    act.wait_ge(scaled_turned, n + 1)
                    stage = bank[n][:]
                act.activation(flat(w[0]), stage, ACT.Copy).then_inc(high_done, 1)

            def step(c, ic):
                s = C_STEPS[c]
                ps = bank[BANK[c]]
                if s[0] == "gram":
                    return
                if s[:3] == ("expand", 3, 1):
                    return
                if s[0] == "corrT":
                    act.wait_ge(c_done, NC * ic + c + 1)
                    act.activation(gsT[:], ps[0:3 * PART, :], ACT.Copy).then_inc(gsT_high, 1)
                    return
                value, high, _ = split_parts(c)
                sc = 1.0
                if s[0] == "expand":
                    _, layer, h, m = s
                    b = col(L3_B3 + m) if layer == 3 else bn[:, 3, 2 + m:3 + m]
                elif s[0] == "mix":
                    _, h, m = s
                    b = col(L1_B + m)
                elif s[0] == "reduce":
                    sc = bn[:, 2, 0:1] if s[1] == 2 else col(L3_S1)
                    b = bn[:, 3, 0:1] if s[1] == 2 else col(L3_B1)
                else:
                    sc = bn[:, 2, 1:2] if s[1] == 2 else col(L3_S2)
                    b = bn[:, 3, 1:2] if s[1] == 2 else col(L3_B2)
                slot_free(act, ic, c)
                act.wait_ge(c_done, NC * ic + c + 1)
                shaped = ps[:] if len(value.shape) == 2 else ps[:].rearrange("p (a b) -> p a b", b=W)
                act.activation(value, shaped, ACT.Relu, bias=b, scale=sc).then_inc(c_drained[BANK[c]], 1)
                if s[:2] == ("expand", 3):
                    return
                act.wait_ge(c_drained[BANK[c]], drains(ic, c) + 1)
                act.activation(high, value, ACT.Copy).then_inc(step_high, 1)

            def body(items, ib, ic):
                for it in items:
                    if it[0] == "a":
                        part_a(it[1], it[2])
                    elif it[0] == "split":
                        split(it[1])
                    elif it[0] == "split corr":
                        act.wait_ge(ld_corr, 48)
                        act.wait_ge(borders_done, 7)
                        for p in range(3):
                            part = slice(PART * p, PART * p + NB)
                            act.activation(l1g[part], corr_stage[part], ACT.Copy).then_inc(corr_high, 1)
                    elif it[0] == "step":
                        step(it[1], ic)
                    elif it[0] == "root":
                        h = it[1]
                        act.wait_ge(norm_asked, 2 * ic + h + 1)
                        act.activation(nrm[:, h, 1, :], nrm[:, h, 0, :], ACT.Sqrt).then_inc(norm_root, 1)
                    elif it[0] == "weigh":
                        _, u, pair = it
                        if pair == 0:
                            if u == 0:
                                act.wait_ge(taken, 2 * ib + 2)
                            wait_past(act, turned, UNITS * ib + u - 1)
                        h, k = u // TAPS, u % TAPS
                        for t in (2 * pair, 2 * pair + 1):
                            n = HT * u + t
                            act.wait_ge(gathered[n % SLOTS], 16 * (UNITS * HT // SLOTS * ib + n // SLOTS + 1))
                            act.activation(samp[:, u % 2, t, :], patch[:, n % SLOTS, 0, :], ACT.Copy,
                                           scale=wgt[:, (HT * h + t) * TAPS + k, 0:1]).then_inc(weighed, 1)
                    elif it[0] == "turn":
                        u = it[1]
                        act.wait_ge(turned, UNITS * ib + u + 1)
                        wait_past(act, tap_done, UNITS * ib + u - 1)
                        wait_past(act, sampT_low, UNITS * ib + u - 1)
                        act.activation(sampT[0][:, u % 2, :], bank[4 + u % 2][:], ACT.Copy).then_inc(sampT_high, 1)
                    elif it[0] == "tap" and it[1] % TAPS == TAPS - 1:
                        u = it[1]
                        h = u // TAPS
                        act.wait_ge(tap_done, UNITS * ib + u + 1)
                        wait_past(act, out0_done, 8 * ib + KC * h)
                        wait_past(act, hid_low, 2 * ib + h)
                        act.activation(hidf[:], bank[6 + h][:], ACT.Relu, bias=col(L0_B2),
                                       scale=col(L0_S2)).then_inc(hid_read, 1)
                        act.wait_ge(hid_read, 2 * ib + h + 1)
                        act.activation(hid[0][:], hidf[:], ACT.Copy).then_inc(hid_high, 1)
                    elif it[0] == "outhigh":
                        _, h, m = it
                        n = 8 * ib + KC * h + m + 1
                        act.wait_ge(res_summed, n)
                        act.activation(res[:, (KC * h + m) % RES, :], res[:, (KC * h + m) % RES, :], ACT.Relu,
                                       bias=col(L0_B3 + m)).then_inc(res_relu, 1)
                        act.wait_ge(res_relu, n)
                        act.activation(x1[0][:, m, PADK + HR * h:PADK + HR * (h + 1), :],
                                       res[:, (KC * h + m) % RES, :].rearrange("p (a b) -> p a b", b=W),
                                       ACT.Copy).then_inc(x1_high, 1)

            act.wait_ge(ld_deform, 32)
            for stage, w, _ in FIRST_SPLITS:
                act.activation(flat(w[0]), stage, ACT.Copy).then_inc(high_done, 1)
            act.wait_ge(bn_done, 5)
            body(PROLOGUE, 0, None)
            for b in range(C_BANKS):
                act.sem_inc(c_drained[b], 1)
            act.wait_ge(borders_done, 9)
            with act.Fori(1, N) as i:
                body(SCHEDULE, i, i - 1)
            body(EPILOGUE, None, N - 1)

        @block.vector
        def _(dve):
            def chain(sem_, base):
                done = [0]

                def link(ins, wait=True):
                    ins.then_inc(sem_, 1)
                    done[0] += 1
                    if wait:
                        dve.wait_ge(sem_, base + done[0])
                return link, done

            link, done = chain(bn_done, 0)
            dve.wait_ge(ld_first, 64)
            dve.tensor_scalar(bn[:, 1, :], prm[:, L2_V:L2_V + 6], BN_EPS, None, ALU.add).then_inc(root_asked, 1)
            dve.wait_ge(root_done, 1)
            dve.wait_ge(root_asked, 1)
            dve.reciprocal(bn[:, 2, :], bn[:, 0, :]).then_inc(root_asked, 1)
            dve.wait_ge(root_asked, 2)
            dve.tensor_tensor(bn[:, 2, :], bn[:, 2, :], bn[:, 1, :], ALU.mult).then_inc(root_asked, 1)
            dve.wait_ge(root_asked, 3)
            link(dve.tensor_tensor(bn[:, 2, :], bn[:, 2, :], bn[:, 0, :], ALU.add))
            link(dve.reciprocal(bn[:, 1, :], bn[:, 2, :]))
            link(dve.scalar_tensor_tensor(bn[:, 2, :], bn[:, 1, :], 2.0, prm[:, L2_G:L2_G + 6], ALU.mult, ALU.mult))
            link(dve.tensor_tensor(bn[:, 3, :], prm[:, L2_M:L2_M + 6], bn[:, 2, :], ALU.mult))
            link(dve.tensor_tensor(bn[:, 3, :], prm[:, L2_B:L2_B + 6], bn[:, 3, :], ALU.subtract))
            dve.wait_ge(iota_done, 7)
            link, done = chain(bn_done, 5)
            link(dve.tensor_scalar(pix[:, 1:2], pix[:, 0:1], 5, None, ALU.arith_shift_right), False)
            link(dve.tensor_scalar(pix[:, 2:3], pix[:, 0:1], W - 1, None, ALU.bitwise_and))
            link(dve.tensor_copy(pixf[:], pix[:, 1:3]))
            for a in range(2):
                link(dve.tensor_scalar(grid[:, :, :, a], grid_i[:, :, :, a], pixf[:, a:a + 1], None, ALU.add), False)
            link(dve.tensor_scalar(band[:], cell_i[:, 0:W, 0], pixf[:, 1:2], None, ALU.subtract), False)
            link(dve.tensor_scalar(col_i[:], col_i[:], FOLD - 1, None, ALU.bitwise_and))
            link(dve.tensor_scalar(wide[:], band[:], float(-PADK), None, ALU.is_ge))
            link(dve.scalar_tensor_tensor(band[:], band[:], float(PADK), wide[:], ALU.is_le, ALU.mult), False)
            link(dve.tensor_scalar(pick[:], col_i[:], 0.0, None, ALU.is_equal), False)
            for dx in range(3):
                for r, rows in enumerate((-W, 0, W, P - W, W - P)):
                    link(dve.tensor_scalar(shifts[:, dx, r, :], dist[:], float(rows + dx - 1), None, ALU.is_equal), False)
            dve.wait_ge(bn_done, 5 + done[0])
            link(dve.memset(shifts[:, 0, :, 0:P:W], 0.0), False)
            link(dve.memset(shifts[:, 2, :, W - 1:P:W], 0.0), False)
            dve.wait_ge(bn_done, 5 + done[0])
            assert done[0] == CONSTS
            for n, (stage, w, _) in enumerate(FIRST_SPLITS):
                dve.wait_ge(high_done, n + 1)
                dve.tensor_tensor(flat(w[1]), stage, flat(w[0]).bitcast(fp32), ALU.subtract).then_inc(low_done, 1)

            def positions(image):
                link, done = chain(a_step, A_STEPS * image)
                NT = TILES * TAPS
                dve.wait_ge(a_done, 8 * image + 8)
                dve.tensor_tensor(pos[:].rearrange("p (t k) a -> p t (k a)", k=TAPS),
                                  bank[3][:, 0:NT * 2].rearrange("p (t o) -> p t o", t=TILES),
                                  offb_t[:].unsqueeze(1).to_broadcast([P, TILES, 2 * TAPS]), ALU.add).then_inc(a_read, 1)
                dve.wait_ge(a_read, image + 1)
                link(dve.tensor_tensor(pos[:], pos[:], grid[:].rearrange("p t k a -> p (t k) a"), ALU.add))
                link(dve.tensor_scalar(cell[:], pos[:], 0.0, float(W - 2), ALU.max, ALU.min))
                link(dve.tensor_copy(cell_i[:], cell[:]))
                link(dve.tensor_copy(far[:], cell_i[:]))
                link(dve.tensor_tensor(hat[:, 0], far[:], cell[:], ALU.is_gt))
                link(dve.tensor_tensor(cell[:], far[:], hat[:, 0], ALU.subtract))
                link(dve.tensor_tensor(far[:], pos[:], cell[:], ALU.subtract))
                link(dve.tensor_scalar(hat[:, 0], far[:], -1.0, 1.0, ALU.mult, ALU.add), False)
                link(dve.tensor_scalar(hat[:, 1], far[:], -1.0, 2.0, ALU.mult, ALU.add))
                link(dve.scalar_tensor_tensor(hat[:, 0], far[:], 1.0, hat[:, 0], ALU.add, ALU.min), False)
                link(dve.tensor_tensor(hat[:, 1], far[:], hat[:, 1], ALU.min))
                link(dve.tensor_scalar(hat[:], hat[:], 0.0, None, ALU.max))
                wv = wgt_all[:, image]
                for dy in range(2):
                    for dx in range(2):
                        link(dve.tensor_tensor(wv[:, :, dy + 2 * dx], hat[:, dy, :, 0], hat[:, dx, :, 1], ALU.mult), False)
                link(dve.scalar_tensor_tensor(entry[:], cell[:, :, 0], float(W), cell[:, :, 1], ALU.mult, ALU.add))
                link(dve.tensor_scalar(idx_all[:, image], entry[:],
                                       float(HW * max(image - 1, 0)), None, ALU.add))
                assert done[0] == A_STEPS

            def gram(g, c, ic):
                h = g // 2
                link, done = chain(corr_step, CORR_STEPS * ic + HALF_STEPS * h + 3 * (g % 2))
                ps = bank[BANK[c]][:].rearrange("p (t r b) -> p t r b", t=2, b=W)
                dve.wait_ge(c_done, NC * ic + c + 1)
                for q in range(RT):
                    rows = slice(W * q, W * (q + 1))
                    ins = dve.tensor_tensor(corr[rows, 2 * (g % 2):2 * (g % 2) + 2, :, :], ps[rows, :, q:q + KS, :],
                                            band[rows].unsqueeze(1).unsqueeze(1).to_broadcast([W, 2, KS, W]), ALU.mult)
                    if q < RT - 1:
                        link(ins, False)
                ins.then_inc(c_drained[BANK[c]], 1)

            def window(h, ic):
                link, done = chain(corr_step, CORR_STEPS * ic + HALF_STEPS * h + 6)
                c = STEP_AT[("gram", 2 * h + 1)]
                for cc in (c - 1, c):
                    dve.wait_ge(c_drained[BANK[cc]], drains(ic, cc) + 1)
                dve.wait_ge(corr_step, CORR_STEPS * ic + HALF_STEPS * h + 6)
                link(dve.tensor_reduce(folded[:], corr[:].rearrange("p t y (g r) -> p (t y) r g", r=FOLD),
                                       AX.X, ALU.add))
                link(dve.tensor_tensor(picked[:], folded[:].unsqueeze(2).to_broadcast([P, HT * KS, KS, FOLD]),
                                       pick[:].unsqueeze(1).to_broadcast([P, HT * KS, KS, FOLD]), ALU.mult))
                gv = raw[:, h]
                link(dve.tensor_reduce(gv.rearrange("p t (y x) -> p (t y) x", x=KS), picked[:], AX.X, ALU.add))
                link(dve.tensor_tensor(gsq[:], gv, gv, ALU.mult))
                link(dve.tensor_reduce(nrm[:, h, 2, :], gsq[:], AX.X, ALU.add))
                dve.tensor_scalar(nrm[:, h, 0, :], nrm[:, h, 2, :], L1_EPS, None, ALU.add).then_inc(norm_asked, 1)

            def normalise(h, ic):
                link, done = chain(corr_step, CORR_STEPS * ic + HALF_STEPS * h + 11)
                total, root, tmp = (nrm[:, h, a, :] for a in range(3))
                dve.wait_ge(norm_asked, 2 * ic + h + 1)
                dve.wait_ge(norm_root, 2 * ic + h + 1)
                link(dve.reciprocal(tmp, root))
                link(dve.tensor_tensor(tmp, tmp, total, ALU.mult))
                link(dve.tensor_tensor(tmp, tmp, root, ALU.add))
                link(dve.reciprocal(root, tmp))
                if h:
                    dve.wait_ge(c_done, NC * ic + STEP_AT[("corrT", 0)] + 1)
                for p in range(3):
                    dve.scalar_tensor_tensor(gs[:, :, p, 0:NB], root.unsqueeze(2).to_broadcast([P, HT, NB]), 2.0,
                                             raw[:, h], ALU.mult, ALU.mult).then_inc(gs_done, 1)

            def body(items, ib, ic):
                for it in items:
                    if it[0] == "positions":
                        positions(it[1])
                    elif it[0] == "scale":
                        stage, w, _, u = SPLITS[it[1]]
                        dve.wait_ge(ld_late[u], 16 * len([s for s in SPLITS if s[3] == u]))
                        for m in range(KC):
                            sc = bn[:, 2, 2 + m:3 + m] if it[1] == 0 else prm[:, L3_S3 + m:L3_S3 + m + 1]
                            v = stage[:, m * P:(m + 1) * P]
                            dve.tensor_scalar(v, v, sc, None, ALU.mult).then_inc(scaled, 1)
                    elif it[0] == "split low" and it[1] == 7:
                        dve.wait_ge(corr_high, 3)
                        part = slice(PART, PART + NB)
                        dve.tensor_tensor(l1g[part], corr_stage[part], l1g[part].bitcast(fp32),
                                          ALU.subtract).then_inc(corr_low, 1)
                    elif it[0] == "split low":
                        stage, w, _, u = SPLITS[it[1]]
                        if it[1] < 2:
                            stage = bank[it[1]][:]
                        dve.wait_ge(high_done, it[1] + 3)
                        if w is l1w:
                            dve.wait_ge(a_step, A_STEPS * N)
                        dve.tensor_tensor(flat(w[1]), stage, flat(w[0]).bitcast(fp32),
                                          ALU.subtract).then_inc(low_done, 1)
                    elif it[0] == "take":
                        wait_past(dve, blended, UNITS * BLEND * ib)
                        wait_past(dve, ticked, 2 * UNITS * ib)
                        dve.tensor_copy(idx[:], idx_all[:, ib]).then_inc(taken, 1)
                        dve.tensor_copy(wgt[:], wgt_all[:, ib]).then_inc(taken, 1)
                        dve.wait_ge(taken, 2 * ib + 2)
                    elif it[0] == "blend":
                        _, u, pair = it
                        h, k = u // TAPS, u % TAPS
                        base = (UNITS * ib + u) * BLEND + 6 * pair
                        for corner in range(1, 4):
                            for tt in range(2):
                                t = 2 * pair + tt
                                w_ = wgt[:, (HT * h + t) * TAPS + k, corner:corner + 1]
                                g_ = patch[:, (HT * u + t) % SLOTS, corner, :]
                                o_ = samp[:, u % 2, t, :]
                                if corner == 1:
                                    dve.wait_ge(weighed, HT * (UNITS * ib + u) + t + 1)
                                else:
                                    dve.wait_ge(blended, base + 2 * corner + tt - 3)
                                dve.scalar_tensor_tensor(o_, g_, w_, o_, ALU.mult, ALU.add).then_inc(blended, 1)
                    elif it[0] == "low":
                        u = it[1]
                        dve.wait_ge(sampT_high, UNITS * ib + u + 1)
                        dve.tensor_tensor(sampT[1][:, u % 2, :], bank[4 + u % 2][:],
                                          sampT[0][:, u % 2, :].bitcast(fp32), ALU.subtract).then_inc(sampT_low, 1)
                    elif it[0] == "hidlow":
                        dve.wait_ge(hid_high, 2 * ib + it[1] + 1)
                        dve.tensor_tensor(hid[1][:], hidf[:], hid[0][:].bitcast(fp32), ALU.subtract).then_inc(hid_low, 1)
                    elif it[0] == "out0":
                        _, h, m = it
                        n = 8 * ib + KC * h + m
                        dve.wait_ge(out0_done, n + 1)
                        slot_ = (KC * h + m) % RES
                        uses = len(range(slot_, 2 * KC, RES))
                        dve.wait_ge(ld_res[slot_], 16 * (uses * ib + (KC * h + m) // RES + 1))
                        dve.scalar_tensor_tensor(res[:, (KC * h + m) % RES, :], bank[out_bank(h, m)][:], prm[:, L0_S3 + m:L0_S3 + m + 1],
                                                 res[:, (KC * h + m) % RES, :], ALU.mult, ALU.add).then_inc(res_summed, 1)
                    elif it[0] == "outlow":
                        _, h, m = it
                        dve.wait_ge(x1_high, 8 * ib + KC * h + m + 1)
                        rows = slice(PADK + HR * h, PADK + HR * (h + 1))
                        dve.tensor_tensor(x1[1][:, m, rows, :], res[:, (KC * h + m) % RES, :].rearrange("p (a b) -> p a b", b=W),
                                          x1[0][:, m, rows, :].bitcast(fp32), ALU.subtract).then_inc(x1_low, 1)
                    elif it[0] == "fine":
                        c = it[1]
                        value, high, low = split_parts(c)
                        dve.wait_ge(step_high, len(SPLIT_STEPS) * ic + HIGH_AT[c] + 1)
                        dve.tensor_tensor(low, value, high.bitcast(fp32), ALU.subtract).then_inc(fine_done, 1)
                    elif it[0] == "step":
                        c = it[1]
                        s = C_STEPS[c]
                        if s[0] == "gram":
                            gram(s[1], c, ic)
                        elif s[:3] == ("expand", 3, 1):
                            slot_free(dve, ic, c)
                            dve.wait_ge(c_done, NC * ic + c + 1)
                            dve.tensor_scalar(slot(c), bank[BANK[c]][:], prm[:, L3_B3 + s[3]:L3_B3 + s[3] + 1], 0.0,
                                              ALU.add, ALU.max).then_inc(c_drained[BANK[c]], 1)
                        elif s[0] == "corrT":
                            dve.wait_ge(gsT_high, 2 * ic + s[1] + 1)
                            dve.tensor_tensor(gsT[2 * PART:3 * PART, :], bank[BANK[c]][2 * PART:3 * PART, :],
                                              gsT[2 * PART:3 * PART, :].bitcast(fp32), ALU.subtract)\
                               .then_inc(c_drained[BANK[c]], 1)
                    elif it[0] == "window":
                        window(it[1], ic)
                    elif it[0] == "normalise":
                        normalise(it[1], ic)

            body(PROLOGUE, 0, None)
            dve.sem_inc(fine_done, 1)
            with dve.Fori(1, N) as i:
                body(SCHEDULE, i, i - 1)
            body(EPILOGUE, None, N - 1)


def kernel(**inputs):
    import numpy as np
    import concourse.bacc as bacc
    from concourse import mybir
    from concourse.bass_utils import run_bass_kernel_spmd

    a = {k: np.asarray(v) for k, v in inputs.items()}

    def lay(w):
        return np.transpose(w.reshape(w.shape[0], w.shape[1], TAPS), (1, 2, 0))

    def chunks(w):
        return np.transpose(w.T.reshape(-1, P, w.shape[0]), (1, 0, 2))

    def cols(*names):
        return [a[n].reshape(-1, P).T for n in names]

    par = np.concatenate(
        cols("L0_conv_bn1_s", "L0_conv_bn1_b", "L0_conv_bn2_s", "L0_conv_bn2_b", "L0_conv_bn3_s", "L0_conv_bn3_b",
             "L1_conv_b")
        + cols(*[f"L2_conv_{v}{n}" for v in "gbmv" for n in (1, 2, 3)])
        + cols("L3_conv_scale1", "L3_conv_bias1", "L3_conv_scale2", "L3_conv_bias2", "L3_conv_scale3",
               "L3_conv_bias3"), axis=1)
    arrays = {
        "x": a["x"],
        "w1t": chunks(a["L0_conv_conv1_w"][:, :, 0, 0]),
        "offwt": lay(a["L0_conv_off_w"]).reshape(P, -1),
        "offb": np.broadcast_to(a["L0_conv_off_b"], (P, 2 * TAPS)),
        "w2t": lay(a["L0_conv_conv2_w"]).reshape(P, -1),
        "w3t": a["L0_conv_conv3_w"][:, :, 0, 0].T,
        "l1wt": chunks(a["L1_conv_W"][:, :C]),
        "l1gt": a["L1_conv_W"][:, C:].T,
        "l2w1t": chunks(a["L2_conv_w1"][:, :, 0, 0]),
        "l2w2t": lay(a["L2_conv_w2"]),
        "l2w3": a["L2_conv_w3"][:, :, 0, 0].reshape(KC, P, P).transpose(1, 0, 2),
        "l3w1t": chunks(a["L3_conv_w1"][:, :, 0, 0]),
        "l3w2t": lay(a["L3_conv_w2"]),
        "l3w3": a["L3_conv_w3"][:, :, 0, 0].reshape(KC, P, P).transpose(1, 0, 2),
        "par": par,
    }
    nc = bacc.Bacc("TRN2", target_bir_lowering=False, num_devices=1)
    given, args = {}, []
    for name, v in arrays.items():
        v = np.ascontiguousarray(v)
        given[f"in_{name}"] = v
        args.append(nc.dram_tensor(f"in_{name}", v.shape, mybir.dt.from_np(v.dtype), kind="ExternalInput").ap())
    out = nc.dram_tensor("out_y", (N, C, H, W), mybir.dt.float32, kind="ExternalOutput").ap()
    conv_seq_kernel(nc, *args, out)
    r = run_bass_kernel_spmd(nc, [given], core_ids=[0])
    return r.results[0]["out_y"]
```

```python
import concourse.bass as bass
from concourse import mybir
from contextlib import ExitStack

N, C, H, W = 4, 512, 32, 32
P = 128
HW = H * W
KC = C // P
HALF = HW // 2
TAPS = 9
TILES = HW // P
RT = P // W
HT = TILES // 2
HR = H // 2
KS = 5
PADK = KS // 2
NB = KS * KS
PART = 32
FOLD = 8
UNITS = 2 * TAPS
OFFS = 2 * TAPS
SLOTS = 12
AHEAD = SLOTS // HT - 1
RES = 3
RING = 4
BLEND = 3 * HT
L1_EPS = 1e-6
BN_EPS = 1e-5

L0_S1, L0_B1, L0_S2, L0_B2, L0_S3, L0_B3 = 0, 1, 2, 3, 4, 8
L1_B = 12
L2_G, L2_B, L2_M, L2_V = 16, 22, 28, 34
L3_S1, L3_B1, L3_S2, L3_B2, L3_S3, L3_B3 = 40, 41, 42, 43, 44, 48
NPAR = 52

C_STEPS = ([("gram", g) for g in range(4)] + [("corrT", 0)] + [("mix", 0, m) for m in range(KC)]
           + [("corrT", 1)] + [("mix", 1, m) for m in range(KC)])
C_STEPS += [("reduce", 2, 0), ("reduce", 2, 1), ("conv", 2, 0), ("expand", 2, 0, 0), ("expand", 2, 0, 1),
            ("conv", 2, 1), ("expand", 2, 0, 2), ("expand", 2, 0, 3), ("expand", 2, 1, 0), ("expand", 2, 1, 1),
            ("reduce", 3, 0), ("expand", 2, 1, 2), ("expand", 2, 1, 3), ("reduce", 3, 1), ("conv", 3, 0),
            ("conv", 3, 1)] + [("expand", 3, h, m) for h in range(2) for m in range(KC)]
NC = len(C_STEPS)
STEP_AT = {s: c for c, s in enumerate(C_STEPS)}
C_BANKS = 4
TAKES = list(C_STEPS)
for h, n in ((0, 2), (1, 2)):
    TAKES.remove(("corrT", h))
    TAKES.insert(TAKES.index(("mix", h, n)), ("corrT", h))
TAKE = [TAKES.index(s) for s in C_STEPS]
BANK = [n % C_BANKS for n in TAKE]
BANK_USES = [BANK.count(b) for b in range(C_BANKS)]
SPLIT_STEPS = [c for c, s in enumerate(C_STEPS) if s[0] not in ("gram", "corrT") and s[:2] != ("expand", 3)]
RING_USE = {c: n for n, c in enumerate(c for c, s in enumerate(C_STEPS) if s[0] not in ("gram", "corrT"))}
A_PARTS = ("conv", "conv", "turn", "turn", "taps", "shift")


def blend_items(u):
    return [("weigh", u, 0), ("weigh", u, 1), ("blend", u, 0), ("blend", u, 1)]


FIRST = [c for c, s in enumerate(C_STEPS) if s[0] == "conv" or (s[0] == "mix" and s[2] < 3)]


def expands(layer, h, first):
    return [("expand", layer, h, m) for m in (first, first + 1)]


ROWS = [([("gram", 0), ("gram", 1), ("window", 0), ("gram", 2), ("root", 0), ("normalise", 0), ("blend", 0),
          ("gram", 3), ("first", "mix", 0, 0), ("first", "mix", 0, 1), ("corrT", 0), ("first", "mix", 0, 2),
          ("window", 1)], None, None),
        ([("mix", 0, 0), ("mix", 0, 1), ("mix", 0, 2)], 0, None),
        ([("mix", 0, 3), ("first", "mix", 1, 0)], 1, None), ([("root", 1), ("normalise", 1)], None, None),
        ([("first", "mix", 1, 1)], 2, None),
        ([("corrT", 1), ("first", "mix", 1, 2)], None, None), ([("mix", 1, 0)], None, None)]
ROWS += [([("mix", 1, m)], 2 + m, None) for m in range(1, KC)]
ROWS += [([("reduce", 2, 0)], 6, None), ([("reduce", 2, 1)], 7, None), ([("first", "conv", 2, 0)], 8, None),
         ([("conv", 2, 0)], 9, None), ([("first", "conv", 2, 1)], 10, None),
         (expands(2, 0, 0), 11, (0, 0)), ([("conv", 2, 1)], 12, None), (expands(2, 0, 2), None, None),
         (expands(2, 1, 0), 13, None), ([("reduce", 3, 0)], 14, None), (expands(2, 1, 2), None, None), ([], 15, (0, 1)),
         ([("reduce", 3, 1)], None, None), ([("first", "conv", 3, 0)], 16, (0, 2)), ([("conv", 3, 0)], 17, (0, 3)),
         ([("first", "conv", 3, 1)], None, None), ([("conv", 3, 1)], None, (1, 0)),
         (expands(3, 0, 0), None, (1, 1)), (expands(3, 0, 2), None, (1, 2)), (expands(3, 1, 0), None, (1, 3)),
         (expands(3, 1, 2), None, None)]


def row_items(middle, u, out, pending):
    items = []
    steps = [it[1] for it in middle if it[0] == "step"]
    if u is not None and u + 1 < UNITS:
        items += blend_items(u + 1)
    items += [("outhigh", *it[1:]) for it in pending if it[0] == "outlow"]
    late = [it for it in pending if it[0] == "outlow"]
    items += middle
    items += [it for it in pending if it[0] == "tap"]
    pending.clear()
    if u is not None:
        items.append(("turn", u))
    if steps and steps[-1] in SPLIT_STEPS:
        items.append(("fine", steps[-1]))
    if middle:
        items += late
        late = []
    if u is not None:
        if u:
            items.append(("tap", u - 1))
        if u == UNITS - 1:
            pending.append(("tap", u))
    if out is not None:
        items += [("out0", *out)] + late
        late = []
        pending.append(("outlow", *out))
    return items + late


def build_schedule():
    items, pending, order = [("take",)], [], []
    for steps, unit, out in ROWS:
        middle, last = [], None
        for s in steps:
            if s[0] == "blend":
                middle += blend_items(s[1])
            elif s[0] == "first":
                middle.append(("first", STEP_AT[s[1:]]))
            elif s in STEP_AT:
                order.append(s)
                middle.append(("step", STEP_AT[s]))
                if last in SPLIT_STEPS:
                    middle.append(("fine", last))
                last = STEP_AT[s]
            else:
                middle.append(s)
        items += row_items(middle, unit, out, pending)
    assert order == C_STEPS
    assert not pending
    return items


def build_prologue():
    items = [("a", 0, k) for k in range(len(A_PARTS))]
    items += [("a", 1, 0), ("a", 1, 1), ("positions", 0), ("take",)] + blend_items(0)
    rows, pending = [], []
    for i in range(1, N):
        if i > 1:
            rows += [[("a", i, 0)], [("positions", i - 1), ("a", i, 1)]]
        rows += [[("a", i, 2), ("a", i, 3), ("a", i, 4)], [("a", i, 5)]]
    rows[-1] += [("scale", 0), ("scale", 1)]
    rows += [[("split", 0), ("split", 1), ("positions", N - 1)],
             [("split low", 0), ("split low", 1), ("split", 2), ("split", 3)],
             [("split low", 2), ("split low", 3), ("split", 4)],
             [("split low", 4), ("split", 5)], [("split", 6)], [("split corr",)]]
    for u in range(UNITS):
        middle = rows.pop(0) if rows else []
        out = (0, u - TAPS - 2) if u in range(TAPS + 2, TAPS + 2 + KC) else None
        items += row_items(middle, u, out, pending)
    items += row_items([], None, None, pending) + [("split low", 5), ("split low", 6)]
    for m in range(KC):
        items += row_items([], None, (1, m), pending) + [("split low", 7)] * (m == 0)
    return items + row_items([], None, None, pending)


SCHEDULE = build_schedule()
PROLOGUE = build_prologue()
EPILOGUE = [it for it in SCHEDULE if it[0] in ("step", "fine", "first", "window", "root", "normalise")]
FINE_AT = {it[1]: n for n, it in enumerate(it for it in SCHEDULE if it[0] == "fine")}
FINES = len(FINE_AT)
assert sorted(FINE_AT) == SPLIT_STEPS


def drains(ic, c):
    return ic * BANK_USES[BANK[c]] + TAKE[c] // C_BANKS + 1


def fined(ic, c):
    return FINES * ic + FINE_AT[c] + 2


def slot_stores(slot):
    return [c for c in RING_USE if C_STEPS[c][:2] == ("expand", 3) and RING_USE[c] % RING == slot]


def wait_past(eng, sem, value):
    if not (isinstance(value, int) and value <= 0):
        eng.wait_ge(sem, value)


def conv_seq_kernel(nc, x, w1t, offwt, offb, w2t, w3t, l1wt, l1gt, l2w1t, l2w2t, l2w3, l3w1t, l3w2t, l3w3,
                    par, out):
    fp32 = mybir.dt.float32
    fp32r = mybir.dt.float32r
    i32 = mybir.dt.int32
    ALU = mybir.AluOpType
    ACT = mybir.ActivationFunctionType
    AX = mybir.AxisListType

    x_v = x.rearrange("n (k p) a b -> n p k (a b)", p=P)
    out_v = out.rearrange("n (k p) a b -> n k p (a b)", p=P)
    table_0 = nc.dram_tensor("patch_table_0", (HW, 2 * P), fp32, kind="Internal")
    table_n = nc.dram_tensor("patch_tables", ((N - 1) * HW, 2 * P), fp32, kind="Internal")
    patches_0, patches_n = table_0.ap()[0:HW - W], table_n.ap()[0:(N - 1) * HW - W]

    ctx = ExitStack()
    with ctx:
        def sb(name, shape, dt=fp32, stack=ctx):
            return stack.enter_context(nc.sbuf_tensor(name, shape, dt))

        def two(name, shape, stack=ctx):
            return [sb(f"{name}_{part}", shape, fp32r, stack) for part in ("high", "low")]

        def sem(name):
            return ctx.enter_context(nc.semaphore(name))

        w2 = sb("w2", [P, TAPS, P])
        w3 = sb("w3", [P, C])
        l1g = sb("l1g", [3 * PART, C], fp32r)
        gs = sb("gs", [P, HT, 3, PART])
        wr = {n: two(f"l{n}w1", [P, KC, P]) for n in (2, 3)}
        wc = {n: two(f"l{n}w2", [P, TAPS, P]) for n in (2, 3)}
        we = {n: two(f"l{n}w3", [P, C]) for n in (2, 3)}
        prm = sb("prm", [P, NPAR])
        bn = sb("bn", [P, 4, 6])
        ident_r = sb("ident_r", [P, P], fp32r)
        ident = ident_r[:].bitcast(fp32)
        band = sb("band", [P, W])
        pick = sb("pick", [P, KS, FOLD])
        idx_all = sb("idx_all", [P, N, TILES * TAPS], i32)
        wgt_all = sb("wgt_all", [P, N, TILES * TAPS, 4])
        tick = sb("tick", [1, 1 + 2 * UNITS])
        idx = sb("idx", [P, TILES * TAPS], i32)
        wgt = sb("wgt", [P, TILES * TAPS, 4])
        patch = sb("patch", [P, SLOTS, 4, P])
        samp = sb("samp", [P, 2, HT, P])
        sampT = sb("sampT", [P, 2, HALF])
        hid = sb("hid", [P, HALF])
        res = sb("res", [P, RES, HALF])
        ring = sb("ring", [P, RING, HALF])
        x1 = two("x1", [P, KC, H + 2 * PADK, W])

        with ExitStack() as early:
            xa = [sb(f"xa{u}", [P, KC, HW], stack=early) for u in range(2)]
            w1 = sb("w1", [P, KC, P], stack=early)
            ident_f = sb("ident_f", [P, P], stack=early)
            wide = sb("wide", [P, W], stack=early)
            offw = sb("offw", [P, TAPS * OFFS], stack=early)
            offb_t = sb("offb_t", [P, OFFS], stack=early)
            mid = sb("mid", [P, HW], stack=early)
            midT = [sb(f"midT{u}", [P, TILES, P], stack=early) for u in range(2)]
            tapped = sb("tapped", [P, TILES, TAPS, OFFS], stack=early)
            dist = sb("dist", [P, P], i32, stack=early)
            shifts = sb("shifts", [P, 3, 5, P], stack=early)
            grid_i = sb("grid_i", [P, TILES, TAPS, 2], i32, stack=early)
            grid = sb("grid", [P, TILES, TAPS, 2], stack=early)
            pix = sb("pix", [P, 4], i32, stack=early)
            pixf = sb("pixf", [P, 2], stack=early)
            col_i = sb("col_i", [P, KS, FOLD], i32, stack=early)
            pos = sb("pos", [P, TILES * TAPS, 2], stack=early)
            cell = sb("cell", [P, TILES * TAPS, 2], stack=early)
            cell_i = sb("cell_i", [P, TILES * TAPS, 2], i32, stack=early)
            far = sb("far", [P, TILES * TAPS, 2], stack=early)
            hat = sb("hat", [P, 2, TILES * TAPS, 2], stack=early)
            entry = sb("entry", [P, TILES * TAPS], stack=early)
        xs = two("xs", [P, KC, HW])
        hp = two("hp", [P, H + 2, W + 2])
        with ExitStack() as layer1:
            corr = sb("corr", [P, 2, HT, KS, W], stack=layer1)
            folded = sb("folded", [P, HT * KS, FOLD], stack=layer1)
            picked = sb("picked", [P, HT * KS, KS, FOLD], stack=layer1)
            gsT = sb("gsT", [3 * PART, HALF], fp32r, stack=layer1)
        h2 = two("h2", [P, 2, HALF])
        sb("layer1_rest", [P, (2 * HT * KS * W + HT * KS * FOLD + HT * KS * KS * FOLD + HALF) - 4 * HALF])
        raw = sb("raw", [P, 2, HT, NB])
        gsq = sb("gsq", [P, HT, NB])
        nrm = sb("nrm", [P, 2, 3, HT])
        l1w = two("l1w", [P, KC, C])

        bank = [ctx.enter_context(nc.psum_tensor(f"bank{b}", [P, HALF], fp32)) for b in range(8)]

        st0 = xa[0][:].rearrange("p k s -> p (k s)")
        st1 = xa[1][:].rearrange("p k s -> p (k s)")
        SPLITS = [(st0[:, 4 * C:5 * C], we[2], l2w3, 0), (st0[:, 5 * C:6 * C], we[3], l3w3, 0),
                  (st1[:, 0:C], wr[2], l2w1t, 1), (st1[:, C:C + TAPS * P], wc[2], l2w2t, 1),
                  (st1[:, C + TAPS * P:2 * C + TAPS * P], wr[3], l3w1t, 1),
                  (st1[:, 2 * C + TAPS * P:2 * C + 2 * TAPS * P], wc[3], l3w2t, 1),
                  (st0[:, 0:4 * C], l1w, l1wt, 0)]
        corr_stage = st1[:, 2 * C + 2 * TAPS * P:3 * C + 2 * TAPS * P]
        def flat(t):
            return t[:].rearrange("p a b -> p (a b)") if len(t.shape) == 3 else t[:]

        ld_first, ld_offset, ld_deform = sem("ld_first"), sem("ld_offset"), sem("ld_deform")
        ld_late = [sem(f"ld_late{u}") for u in range(2)]
        ld_corr = sem("ld_corr")
        ld_x0 = [sem(f"ld_x0_{k}") for k in range(KC)]
        ld_xa = [sem(f"ld_xa{n}") for n in range(4)]
        iota_done, const_done, borders_done = sem("iota_done"), sem("const_done"), sem("borders_done")
        root_asked, root_done, bn_done = sem("root_asked"), sem("root_done"), sem("bn_done")
        a_done, a_drained, a_step, a_read = sem("a_done"), sem("a_drained"), sem("a_step"), sem("a_read")
        high_done, low_done = sem("high_done"), sem("low_done")
        tabled = [sem(f"tabled{u}") for u in range(2)]
        taken, ticked = sem("taken"), sem("ticked")
        gathered = [sem(f"gathered{s}") for s in range(SLOTS)]
        blended = sem("blended")
        turned, sampT_done, tap_done, hid_done = (sem(n) for n in ("turned", "sampT_done", "tap_done", "hid_done"))
        out0_done, res_summed, res_relu, x1_high, x1_low = (
            sem(n) for n in ("out0_done", "res_summed", "res_relu", "x1_high", "x1_low"))
        ld_res = [sem(f"ld_res{n}") for n in range(RES)]
        c_done = sem("c_done")
        c_drained = [sem(f"c_drained{b}") for b in range(C_BANKS)]
        corr_step, norm_asked, norm_root, gs_done = (
            sem(n) for n in ("corr_step", "norm_asked", "norm_root", "gs_done"))
        step_high, fine_done = sem("step_high"), sem("fine_done")
        stored = [sem(f"stored{n}") for n in range(RING)]
        weighed, aligned = sem("weighed"), sem("aligned")
        gsT_high, corr_high, corr_low = sem("gsT_high"), sem("corr_high"), sem("corr_low")
        scaled, scaled_turned, ident_done = sem("scaled"), sem("scaled_turned"), sem("ident_done")

        block = ctx.enter_context(nc.Block())

        CONSTS = 27
        A_STEPS = 18
        HALF_STEPS = 10
        CORR_STEPS = 20
        FIRST_TAPS = 6
        HIGH_AT = {c: n for n, c in enumerate(SPLIT_STEPS)}

        def out_bank(h, m):
            return 6 + (h + m) % 2 if h else 6

        def slot(c):
            return ring[:, RING_USE[c] % RING, :]

        def table_dmas(parity, images):
            return 16 * sum(5 if i < 2 else 4 for i in range(parity, images, 2))

        def slot_free(eng, ic, c):
            n = RING_USE[c] - RING
            before = [x for x in RING_USE if RING_USE[x] == n]
            mine = slot_stores(n % RING)
            if n < 0:
                eng.wait_ge(stored[n % RING], 16 * len(mine) * ic + 1)
            elif before[0] in SPLIT_STEPS:
                eng.wait_ge(fine_done, fined(ic, before[0]))
            else:
                eng.wait_ge(stored[n % RING], 16 * (len(mine) * ic + mine.index(before[0]) + 1) + 1)

        def split_parts(c):
            s = C_STEPS[c]
            if s[0] in ("mix", "expand"):
                h, m = s[-2:]
                return slot(c), *(xs[p][:, m, h * HALF:(h + 1) * HALF] for p in range(2))
            if s[0] == "reduce":
                rows = slice(1 + HR * s[2], 1 + HR * (s[2] + 1))
                return slot(c).rearrange("p (a b) -> p a b", b=W), *(hp[p][:, rows, 1:W + 1] for p in range(2))
            return slot(c), *(h2[p][:, s[2], :] for p in range(2))

        @block.sync
        def _(sp):
            def load_x(i, h):
                sp.dma_start(xa[i % 2][:, :, h * HALF:(h + 1) * HALF],
                             x_v[i, :, :, h * HALF:(h + 1) * HALF]).then_inc(ld_xa[2 * (i % 2) + h], 16)

            sp.dma_start(w1[:], w1t).then_inc(ld_first, 16)
            sp.dma_start(prm[:], par).then_inc(ld_first, 16)
            for k in range(KC):
                sp.dma_start(xa[0][:, k, 0:HALF], x_v[0, :, k, 0:HALF]).then_inc(ld_x0[k], 16)
            load_x(0, 1)
            for t, d in ((offw, offwt), (offb_t, offb)):
                sp.dma_start(t[:], d).then_inc(ld_offset, 16)
            sp.dma_start(flat(w2), w2t).then_inc(ld_deform, 16)
            sp.dma_start(w3[:], w3t).then_inc(ld_deform, 16)
            load_x(1, 0)
            load_x(1, 1)
            def load_res(n, ib):
                h, m = n // KC, n % KC
                if n == 0:
                    wait_past(sp, x1_low, 8 * ib)
                elif n >= RES:
                    sp.wait_ge(x1_low, 8 * ib + n - RES + 1)
                sp.dma_start(res[:, n % RES, :], x_v[ib, :, m, h * HALF:(h + 1) * HALF]).then_inc(ld_res[n % RES], 16)

            def body(items, ib, ic):
                if ib is not None:
                    for n in range(RES):
                        load_res(n, ib)
                for it in items:
                    if it[0] == "a":
                        _, i, k = it
                        if k in (1, 3) and 1 <= i < N - 1:
                            sp.wait_ge(a_done, 8 * (i - 1) + 2)
                            load_x(i + 1, k // 2)
                        if k == 3 and i >= N - 2:
                            sp.wait_ge(a_done, 8 * i + 2)
                            for stage, _, d, u in SPLITS:
                                if u == i % 2:
                                    sp.dma_start(stage, d if len(d.shape) == 2 else d.rearrange("p a b -> p (a b)"))\
                                      .then_inc(ld_late[u], 16)
                            if i == N - 1:
                                for p in range(3):
                                    sp.dma_start(corr_stage[PART * p:PART * p + NB], l1gt).then_inc(ld_corr, 16)
                        if A_PARTS[k] == "turn":
                            h = k - 2
                            sp.wait_ge(a_drained, 7 * i + 3 + h)
                            table = (table_n if i else table_0).ap()
                            pixels = midT[i % 2]
                            done = tabled[i % 2]
                            for above in range(2):
                                first = HW * max(i - 1, 0) + HALF * h - above * W
                                cols = slice(above * P, (above + 1) * P)
                                tiles = HT
                                if first < 0:
                                    sp.dma_start(table[0:P - W, cols], pixels[W:P, 0, :]).then_inc(done, 16)
                                    first, tiles = P - W, HT - 1
                                sp.dma_start(table[first:first + tiles * P, cols].rearrange("(t p) c -> p t c", p=P),
                                             pixels[:, HT * h + HT - tiles:HT * h + HT, :]).then_inc(done, 16)
                    if it[0] == "outlow" and KC * it[1] + it[2] + RES < 2 * KC:
                        load_res(KC * it[1] + it[2] + RES, ib)
                    if it[0] == "step" and C_STEPS[it[1]][:2] == ("expand", 3):
                        _, _, h, m = C_STEPS[it[1]]
                        c = it[1]
                        sp.wait_ge(c_drained[BANK[c]], drains(ic, c) + 1)
                        sp.dma_start(out_v[ic, m, :, h * HALF:(h + 1) * HALF], slot(c))\
                          .then_inc(stored[RING_USE[c] % RING], 16)

            body(PROLOGUE, 0, None)
            for n in range(RING):
                sp.sem_inc(stored[n], 1)
            with sp.Fori(1, N) as i:
                body(SCHEDULE, i, i - 1)
            body(EPILOGUE, None, N - 1)
            for n in range(RING):
                sp.wait_ge(stored[n], 16 * len(slot_stores(n)) * N + 1)

        @block.gpsimd
        def _(pool):
            pool.iota(pix[:, 0:1], [[0, 1]], base=0, channel_multiplier=1).then_inc(iota_done, 1)
            pool.iota(dist[:], [[-1, P]], base=0, channel_multiplier=1).then_inc(iota_done, 1)
            pool.iota(grid_i[:, :, :, 0].rearrange("p t (a b) -> p t a b", b=3), [[RT, TILES], [1, 3], [0, 3]],
                      base=-1, channel_multiplier=0).then_inc(iota_done, 1)
            pool.iota(grid_i[:, :, :, 1].rearrange("p t (a b) -> p t a b", b=3), [[0, TILES], [0, 3], [1, 3]],
                      base=-1, channel_multiplier=0).then_inc(iota_done, 1)
            pool.iota(col_i[:, :, :], [[1, KS], [-1, FOLD]], base=2 * FOLD - PADK, channel_multiplier=1)\
                .then_inc(iota_done, 1)
            pool.iota(cell_i[:, 0:W, 0], [[1, W]], base=0, channel_multiplier=0).then_inc(iota_done, 1)
            pool.memset(ident_f[:], 0.0).then_inc(iota_done, 1)
            pool.wait_ge(iota_done, 7)
            pool.affine_select(out=ident_f[:], in_=ident_f[:], compare_op=ALU.not_equal, fill=1.0, base=0,
                               pattern=[[-1, P]], channel_multiplier=1).then_inc(const_done, 1)
            pool.memset(tick[:], 0.0).then_inc(borders_done, 1)
            pool.memset(l1g[:].bitcast(fp32), 0.0).then_inc(borders_done, 1)
            pool.memset(gs[:], 0.0).then_inc(borders_done, 1)
            for part in range(2):
                pool.memset(x1[part][:, :, 0:PADK, :].bitcast(fp32), 0.0).then_inc(borders_done, 1)
                pool.memset(x1[part][:, :, H + PADK:, :].bitcast(fp32), 0.0).then_inc(borders_done, 1)
            pool.wait_ge(borders_done, 7)
            pool.wait_ge(tabled[0], table_dmas(0, 1))

            def freed_by(n):
                u, t = n // HT, n % HT
                return u * BLEND + 6 * (t // 2) + 6

            def gather(u, ib):
                table = patches_0 if isinstance(ib, int) else patches_n
                h, k = u // TAPS, u % TAPS
                for t in range(HT):
                    n = HT * u + t
                    if t % 2 == 0:
                        wait_past(pool, blended, UNITS * BLEND * ib + freed_by(n - SLOTS))
                        p = 1 + 2 * u + t // 2
                        pool.tensor_tensor(tick[:, p:p + 1], tick[:, 0:1], tick[:, 0:1], ALU.add).then_inc(ticked, 1)
                    e = (HT * h + t) * TAPS + k
                    pool.indirect_dma_start(patch[:, n % SLOTS].rearrange("p a c -> p (a c)"), None, table,
                                            bass.IndirectOffsetOnAxis(ap=idx[:, e:e + 1], axis=0))\
                        .then_inc(gathered[n % SLOTS], 16)

            def body(items, ib, ic):
                for it in items:
                    if it[0] == "take":
                        wait_past(pool, ticked, 2 * UNITS * ib)
                        pool.wait_ge(taken, 2 * ib + 2)
                        for u in range(AHEAD):
                            gather(u, ib)
                    if it[0] == "blend" and it[1] + AHEAD < UNITS and it[2] == 0:
                        gather(it[1] + AHEAD, ib)

            body(PROLOGUE, 0, None)
            pool.wait_ge(a_done, 8 * N)
            pool.wait_ge(a_drained, 7 * N)
            pool.wait_ge(a_step, A_STEPS * N)
            pool.wait_ge(tabled[0], table_dmas(0, N))
            pool.wait_ge(tabled[1], table_dmas(1, N))
            pool.wait_ge(low_done, 7)
            for part in range(2):
                pool.memset(hp[part][:].bitcast(fp32), 0.0).then_inc(borders_done, 1)
            with pool.Fori(1, N) as i:
                body(SCHEDULE, i, i - 1)

        @block.tensor
        def _(pe):
            def product(ps, w, a, start, stop):
                pe.matmul(ps, w[0], a[0], start=start, stop=False)
                pe.matmul(ps, w[0], a[1], start=False, stop=False)
                return pe.matmul(ps, w[1], a[0], start=False, stop=stop)

            pe.wait_ge(ld_first, 32)
            pe.wait_ge(ident_done, 1)

            def part_a(i, k):
                if A_PARTS[k] == "conv":
                    h = k
                    if (i, h) != (0, 0):
                        pe.wait_ge(ld_xa[2 * (i % 2) + h], 16 * (i // 2 + max(i % 2, h)))
                    wait_past(pe, a_drained, 7 * (i - 1) + 5 + h)
                    for c in range(KC):
                        if (i, h) == (0, 0):
                            pe.wait_ge(ld_x0[c], 16)
                        last = pe.matmul(bank[h][:], w1[:, c, :], xa[i % 2][:, c, h * HALF:(h + 1) * HALF],
                                         start=c == 0, stop=c == KC - 1)
                    last.then_inc(a_done, 1)
                elif A_PARTS[k] == "turn":
                    h = k - 2
                    pe.wait_ge(a_drained, 7 * i + h + 1)
                    wait_past(pe, a_drained, 7 * i)
                    wait_past(pe, a_read, i)
                    for t in range(HT):
                        last = pe.transpose(bank[2 + h][:, t * P:(t + 1) * P],
                                            mid[:, (HT * h + t) * P:(HT * h + t + 1) * P], ident)
                    last.then_inc(a_done, 1)
                elif A_PARTS[k] == "taps":
                    pe.wait_ge(ld_offset, 32)
                    for g in range(3):
                        tiles = range(3 * g, min(3 * g + 3, TILES))
                        pe.wait_ge(a_drained, 7 * i + (2, 2, 3)[g])
                        for t in tiles:
                            last = pe.matmul(bank[g][:, (t - 3 * g) * TAPS * OFFS:(t - 3 * g + 1) * TAPS * OFFS],
                                             mid[:, t * P:(t + 1) * P], offw[:], start=True, stop=True)
                        last.then_inc(a_done, 1)
                else:
                    pe.wait_ge(a_drained, 7 * i + 7)
                    pe.wait_ge(bn_done, 5 + CONSTS)
                    ps = bank[3][:, 0:TILES * OFFS]
                    for tap in range(TAPS):
                        pe.matmul(ps, shifts[:, tap % 3, tap // 3, :], tapped[:, :, tap, :],
                                  start=tap == 0, stop=False)
                    for row, r in ((0, 3), (2, 4)):
                        n = (TILES - 1) * OFFS
                        to, frm = (OFFS, 0) if row == 0 else (0, 1)
                        for col in range(3):
                            last = pe.matmul(ps[:, to:to + n], shifts[:, col, r, :],
                                             tapped[:, frm:frm + TILES - 1, 3 * row + col, :],
                                             start=False, stop=(row, col) == (2, 2))
                    last.then_inc(a_done, 1)

            def first(c, ic):
                s = C_STEPS[c]
                ps = bank[BANK[c]]
                pe.wait_ge(c_drained[BANK[c]], drains(ic, c))
                if s[0] == "mix":
                    _, h, m = s
                    for k in range(KC):
                        product(ps[:], [l1w[p][:, k, m * P:(m + 1) * P] for p in range(2)],
                                [x1[p][:, k, PADK + HR * h:PADK + HR * (h + 1), :] for p in range(2)], k == 0, False)
                else:
                    pe.wait_ge(fine_done, fined(ic, STEP_AT[("reduce", s[1], s[2])]))
                    conv_taps(c, range(FIRST_TAPS))

            def conv_taps(c, taps):
                _, layer, h = C_STEPS[c]
                for k in taps:
                    row, col = HR * h + k // 3, k % 3
                    last = product(bank[BANK[c]][:], [wc[layer][p][:, k, :] for p in range(2)],
                                   [hp[p][:, row:row + HR, col:col + W] for p in range(2)], k == 0, k == TAPS - 1)
                return last

            def step(c, ic):
                s = C_STEPS[c]
                ps = bank[BANK[c]]
                if s[0] == "mix" and c not in FIRST:
                    first(c, ic)
                elif c not in FIRST:
                    pe.wait_ge(c_drained[BANK[c]], drains(ic, c))
                if s[0] == "gram":
                    if s[1] < 2:
                        pe.wait_ge(x1_low, 8 * ic + KC * (s[1] + 1))
                    for half in range(2):
                        t = 2 * s[1] + half
                        for k in range(KC):
                            own = [x1[p][:, k, RT * t + PADK:RT * t + PADK + RT, :] for p in range(2)]
                            near = [x1[p][:, k, RT * t:RT * t + 2 * RT, :] for p in range(2)]
                            last = product(ps[:, half * 2 * P:(half + 1) * 2 * P], own, near, k == 0, k == KC - 1)
                elif s[0] == "corrT":
                    h = s[1]
                    pe.wait_ge(gs_done, 6 * ic + 3 * h + 3)
                    for t in range(HT):
                        last = pe.transpose(ps[0:3 * PART, t * P:(t + 1) * P],
                                            gs[:, t].rearrange("p a b -> p (a b)"), ident)
                elif s[0] == "mix":
                    _, h, m = s
                    ct = STEP_AT[("corrT", h)]
                    pe.wait_ge(c_drained[BANK[ct]], drains(ic, ct) + 1)
                    last = pe.matmul(ps[:], l1g[:, m * P:(m + 1) * P], gsT[:], start=False, stop=True)
                elif s[0] == "reduce":
                    _, layer, h = s
                    source = [STEP_AT[("mix", h, m) if layer == 2 else ("expand", 2, h, m)] for m in range(KC)]
                    pe.wait_ge(fine_done, fined(ic, max(source, key=FINE_AT.get)))
                    for k in range(KC):
                        last = product(ps[:], [wr[layer][p][:, k, :] for p in range(2)],
                                       [xs[p][:, k, h * HALF:(h + 1) * HALF] for p in range(2)], k == 0, k == KC - 1)
                elif s[0] == "conv":
                    _, layer, h = s
                    pe.wait_ge(fine_done, fined(ic, STEP_AT[("reduce", layer, 1)]))
                    last = conv_taps(c, range(FIRST_TAPS, TAPS))
                elif s[0] == "expand":
                    _, layer, h, m = s
                    pe.wait_ge(fine_done, fined(ic, STEP_AT[("conv", layer, h)]))
                    for p in range(2):
                        pe.matmul(ps[:], ident_r[:], xs[p][:, m, h * HALF:(h + 1) * HALF], start=p == 0, stop=False)
                    last = product(ps[:], [we[layer][p][:, m * P:(m + 1) * P] for p in range(2)],
                                   [h2[p][:, h, :] for p in range(2)], False, True)
                last.then_inc(c_done, 1)

            def body(items, ib, ic):
                for it in items:
                    if it[0] == "a":
                        part_a(it[1], it[2])
                    elif it[0] == "split" and it[1] < 2:
                        pe.wait_ge(scaled, KC * (it[1] + 1))
                        pe.wait_ge(a_drained, 7 * N)
                        for m in range(KC):
                            last = pe.transpose(bank[it[1]][:, m * P:(m + 1) * P],
                                                SPLITS[it[1]][0][:, m * P:(m + 1) * P], ident)
                        last.then_inc(scaled_turned, 1)
                    elif it[0] == "first":
                        first(it[1], ic)
                    elif it[0] == "step":
                        step(it[1], ic)
                    elif it[0] == "turn":
                        u = it[1]
                        pe.wait_ge(blended, (UNITS * ib + u + 1) * BLEND)
                        wait_past(pe, sampT_done, UNITS * ib + u - 1)
                        for t in range(HT):
                            last = pe.transpose(bank[4 + u % 2][:, t * P:(t + 1) * P], samp[:, u % 2, t, :], ident)
                        last.then_inc(turned, 1)
                    elif it[0] == "tap":
                        u = it[1]
                        h, k = u // TAPS, u % TAPS
                        if k == 0:
                            wait_past(pe, res_summed, 8 * ib)
                        if u == 0 and isinstance(ib, int):
                            pe.wait_ge(ld_deform, 32)
                        pe.wait_ge(sampT_done, UNITS * ib + u + 1)
                        pe.matmul(bank[6 + h][:], w2[:, k, :], sampT[:, u % 2, :],
                                  start=k == 0, stop=k == TAPS - 1).then_inc(tap_done, 1)
                    elif it[0] == "out0":
                        _, h, m = it
                        pe.wait_ge(hid_done, 2 * ib + h + 1)
                        b = out_bank(h, m)
                        if h == 1 and m == 1:
                            pe.wait_ge(res_summed, 8 * ib + KC)
                        elif m:
                            pe.wait_ge(res_summed, 8 * ib + KC * h + m - h)
                        pe.matmul(bank[b][:], w3[:, m * P:(m + 1) * P], hid[:], start=True, stop=True)\
                            .then_inc(out0_done, 1)

            body(PROLOGUE, 0, None)
            pe.wait_ge(corr_low, 1)
            pe.wait_ge(borders_done, 9)
            pe.wait_ge(ident_done, 1)
            pe.wait_ge(low_done, 7)
            with pe.Fori(1, N) as i:
                body(SCHEDULE, i, i - 1)
            body(EPILOGUE, None, N - 1)

        @block.scalar
        def _(act):
            def col(n):
                return prm[:, n:n + 1]

            act.wait_ge(const_done, 1)
            act.activation(ident_r[:], ident_f[:], ACT.Copy).then_inc(ident_done, 1)
            act.wait_ge(ld_first, 32)
            act.wait_ge(root_asked, 1)
            act.activation(bn[:, 0, :], bn[:, 1, :], ACT.Sqrt).then_inc(root_done, 1)

            def part_a(i, k):
                if A_PARTS[k] == "conv":
                    act.wait_ge(a_done, 8 * i + k + 1)
                    act.activation(mid[:, k * HALF:(k + 1) * HALF], bank[k][:], ACT.Relu,
                                   bias=col(L0_B1), scale=col(L0_S1)).then_inc(a_drained, 1)
                elif A_PARTS[k] == "turn":
                    h = k - 2
                    act.wait_ge(a_done, 8 * i + k + 1)
                    wait_past(act, tabled[i % 2], table_dmas(i % 2, i))
                    act.activation(midT[i % 2][:, HT * h:HT * (h + 1), :],
                                   bank[2 + h][:].rearrange("p (t c) -> p t c", c=P), ACT.Copy).then_inc(a_drained, 1)
                elif A_PARTS[k] == "taps":
                    wait_past(act, a_done, 8 * i)
                    for g in range(3):
                        n = min(3, TILES - 3 * g)
                        act.wait_ge(a_done, 8 * i + 5 + g)
                        act.activation(tapped[:, 3 * g:3 * g + n].rearrange("p t k o -> p (t k o)"),
                                       bank[g][:, 0:n * TAPS * OFFS], ACT.Copy).then_inc(a_drained, 1)

            def split(n):
                stage, w, _, u = SPLITS[n]
                act.wait_ge(ld_late[u], 16 * len([s for s in SPLITS if s[3] == u]))
                if w is l1w:
                    act.wait_ge(a_step, A_STEPS * N)
                    act.wait_ge(tabled[0], table_dmas(0, N))
                    act.wait_ge(tabled[1], table_dmas(1, N))
                if n < 2:
                    act.wait_ge(scaled_turned, n + 1)
                    stage = bank[n][:]
                act.activation(flat(w[0]), stage, ACT.Copy).then_inc(high_done, 1)

            def step(c, ic):
                s = C_STEPS[c]
                ps = bank[BANK[c]]
                if s[0] == "gram":
                    g = s[1]
                    rows_ps = ps[:].rearrange("p (t r b) -> p t r b", t=2, b=W)
                    act.wait_ge(c_done, NC * ic + c + 1)
                    for q in range(RT):
                        rows = slice(W * q, W * (q + 1))
                        ins = act.activation(corr[rows, g // 2, 2 * (g % 2):2 * (g % 2) + 2, :, :],
                                             rows_ps[rows, :, q:q + KS, :], ACT.Copy)
                        if q < RT - 1:
                            ins.then_inc(aligned, 1)
                    ins.then_inc(c_drained[BANK[c]], 1)
                    return
                if s[:3] == ("expand", 3, 1):
                    return
                if s[0] == "corrT":
                    act.wait_ge(c_done, NC * ic + c + 1)
                    act.activation(gsT[:], ps[0:3 * PART, :], ACT.Copy).then_inc(gsT_high, 1)
                    return
                value, high, _ = split_parts(c)
                sc = 1.0
                if s[0] == "expand":
                    _, layer, h, m = s
                    b = col(L3_B3 + m) if layer == 3 else bn[:, 3, 2 + m:3 + m]
                elif s[0] == "mix":
                    _, h, m = s
                    b = col(L1_B + m)
                elif s[0] == "reduce":
                    sc = bn[:, 2, 0:1] if s[1] == 2 else col(L3_S1)
                    b = bn[:, 3, 0:1] if s[1] == 2 else col(L3_B1)
                else:
                    sc = bn[:, 2, 1:2] if s[1] == 2 else col(L3_S2)
                    b = bn[:, 3, 1:2] if s[1] == 2 else col(L3_B2)
                slot_free(act, ic, c)
                act.wait_ge(c_done, NC * ic + c + 1)
                shaped = ps[:] if len(value.shape) == 2 else ps[:].rearrange("p (a b) -> p a b", b=W)
                act.activation(value, shaped, ACT.Relu, bias=b, scale=sc).then_inc(c_drained[BANK[c]], 1)
                if s[:2] == ("expand", 3):
                    return
                act.wait_ge(c_drained[BANK[c]], drains(ic, c) + 1)
                act.activation(high, value, ACT.Copy).then_inc(step_high, 1)

            def body(items, ib, ic):
                for it in items:
                    if it[0] == "a":
                        part_a(it[1], it[2])
                    elif it[0] == "split":
                        split(it[1])
                    elif it[0] == "split corr":
                        act.wait_ge(ld_corr, 48)
                        act.wait_ge(borders_done, 7)
                        for p in range(3):
                            part = slice(PART * p, PART * p + NB)
                            act.activation(l1g[part], corr_stage[part], ACT.Copy).then_inc(corr_high, 1)
                    elif it[0] == "step":
                        step(it[1], ic)
                    elif it[0] == "root":
                        h = it[1]
                        act.wait_ge(norm_asked, 2 * ic + h + 1)
                        act.activation(nrm[:, h, 1, :], nrm[:, h, 0, :], ACT.Sqrt).then_inc(norm_root, 1)
                    elif it[0] == "weigh":
                        _, u, pair = it
                        if pair == 0:
                            if u == 0:
                                act.wait_ge(taken, 2 * ib + 2)
                            wait_past(act, turned, UNITS * ib + u - 1)
                        h, k = u // TAPS, u % TAPS
                        for t in (2 * pair, 2 * pair + 1):
                            n = HT * u + t
                            act.wait_ge(gathered[n % SLOTS], 16 * (UNITS * HT // SLOTS * ib + n // SLOTS + 1))
                            act.activation(samp[:, u % 2, t, :], patch[:, n % SLOTS, 0, :], ACT.Copy,
                                           scale=wgt[:, (HT * h + t) * TAPS + k, 0:1]).then_inc(weighed, 1)
                    elif it[0] == "turn":
                        u = it[1]
                        act.wait_ge(turned, UNITS * ib + u + 1)
                        wait_past(act, tap_done, UNITS * ib + u - 1)
                        act.activation(sampT[:, u % 2, :], bank[4 + u % 2][:], ACT.Copy).then_inc(sampT_done, 1)
                    elif it[0] == "tap" and it[1] % TAPS == TAPS - 1:
                        u = it[1]
                        h = u // TAPS
                        act.wait_ge(tap_done, UNITS * ib + u + 1)
                        wait_past(act, out0_done, 8 * ib + KC * h)
                        act.activation(hid[:], bank[6 + h][:], ACT.Relu, bias=col(L0_B2),
                                       scale=col(L0_S2)).then_inc(hid_done, 1)
                    elif it[0] == "outhigh":
                        _, h, m = it
                        n = 8 * ib + KC * h + m + 1
                        act.wait_ge(res_summed, n)
                        act.activation(res[:, (KC * h + m) % RES, :], res[:, (KC * h + m) % RES, :], ACT.Relu,
                                       bias=col(L0_B3 + m)).then_inc(res_relu, 1)
                        act.wait_ge(res_relu, n)
                        act.activation(x1[0][:, m, PADK + HR * h:PADK + HR * (h + 1), :],
                                       res[:, (KC * h + m) % RES, :].rearrange("p (a b) -> p a b", b=W),
                                       ACT.Copy).then_inc(x1_high, 1)

            act.wait_ge(bn_done, 5)
            body(PROLOGUE, 0, None)
            for b in range(C_BANKS):
                act.sem_inc(c_drained[b], 1)
            act.wait_ge(borders_done, 9)
            with act.Fori(1, N) as i:
                body(SCHEDULE, i, i - 1)
            body(EPILOGUE, None, N - 1)

        @block.vector
        def _(dve):
            def chain(sem_, base):
                done = [0]

                def link(ins, wait=True):
                    ins.then_inc(sem_, 1)
                    done[0] += 1
                    if wait:
                        dve.wait_ge(sem_, base + done[0])
                return link, done

            link, done = chain(bn_done, 0)
            dve.wait_ge(ld_first, 32)
            dve.tensor_scalar(bn[:, 1, :], prm[:, L2_V:L2_V + 6], BN_EPS, None, ALU.add).then_inc(root_asked, 1)
            dve.wait_ge(root_done, 1)
            dve.wait_ge(root_asked, 1)
            dve.reciprocal(bn[:, 2, :], bn[:, 0, :]).then_inc(root_asked, 1)
            dve.wait_ge(root_asked, 2)
            dve.tensor_tensor(bn[:, 2, :], bn[:, 2, :], bn[:, 1, :], ALU.mult).then_inc(root_asked, 1)
            dve.wait_ge(root_asked, 3)
            link(dve.tensor_tensor(bn[:, 2, :], bn[:, 2, :], bn[:, 0, :], ALU.add))
            link(dve.reciprocal(bn[:, 1, :], bn[:, 2, :]))
            link(dve.scalar_tensor_tensor(bn[:, 2, :], bn[:, 1, :], 2.0, prm[:, L2_G:L2_G + 6], ALU.mult, ALU.mult))
            link(dve.tensor_tensor(bn[:, 3, :], prm[:, L2_M:L2_M + 6], bn[:, 2, :], ALU.mult))
            link(dve.tensor_tensor(bn[:, 3, :], prm[:, L2_B:L2_B + 6], bn[:, 3, :], ALU.subtract))
            dve.wait_ge(iota_done, 7)
            link, done = chain(bn_done, 5)
            link(dve.tensor_scalar(pix[:, 1:2], pix[:, 0:1], 5, None, ALU.arith_shift_right), False)
            link(dve.tensor_scalar(pix[:, 2:3], pix[:, 0:1], W - 1, None, ALU.bitwise_and))
            link(dve.tensor_copy(pixf[:], pix[:, 1:3]))
            for a in range(2):
                link(dve.tensor_scalar(grid[:, :, :, a], grid_i[:, :, :, a], pixf[:, a:a + 1], None, ALU.add), False)
            link(dve.tensor_scalar(band[:], cell_i[:, 0:W, 0], pixf[:, 1:2], None, ALU.subtract), False)
            link(dve.tensor_scalar(col_i[:], col_i[:], FOLD - 1, None, ALU.bitwise_and))
            link(dve.tensor_scalar(wide[:], band[:], float(-PADK), None, ALU.is_ge))
            link(dve.scalar_tensor_tensor(band[:], band[:], float(PADK), wide[:], ALU.is_le, ALU.mult), False)
            link(dve.tensor_scalar(pick[:], col_i[:], 0.0, None, ALU.is_equal), False)
            for dx in range(3):
                for r, rows in enumerate((-W, 0, W, P - W, W - P)):
                    link(dve.tensor_scalar(shifts[:, dx, r, :], dist[:], float(rows + dx - 1), None,
                                           ALU.is_equal), False)
            dve.wait_ge(bn_done, 5 + done[0])
            link(dve.memset(shifts[:, 0, :, 0:P:W], 0.0), False)
            link(dve.memset(shifts[:, 2, :, W - 1:P:W], 0.0), False)
            dve.wait_ge(bn_done, 5 + done[0])
            assert done[0] == CONSTS
            def positions(image):
                link, done = chain(a_step, A_STEPS * image)
                NT = TILES * TAPS
                dve.wait_ge(ld_offset, 32)
                dve.wait_ge(a_done, 8 * image + 8)
                dve.tensor_tensor(pos[:].rearrange("p (t k) a -> p t (k a)", k=TAPS),
                                  bank[3][:, 0:NT * 2].rearrange("p (t o) -> p t o", t=TILES),
                                  offb_t[:].unsqueeze(1).to_broadcast([P, TILES, 2 * TAPS]),
                                  ALU.add).then_inc(a_read, 1)
                dve.wait_ge(a_read, image + 1)
                link(dve.tensor_tensor(pos[:], pos[:], grid[:].rearrange("p t k a -> p (t k) a"), ALU.add))
                link(dve.tensor_scalar(cell[:], pos[:], 0.0, float(W - 2), ALU.max, ALU.min))
                link(dve.tensor_copy(cell_i[:], cell[:]))
                link(dve.tensor_copy(far[:], cell_i[:]))
                link(dve.tensor_tensor(hat[:, 0], far[:], cell[:], ALU.is_gt))
                link(dve.tensor_tensor(cell[:], far[:], hat[:, 0], ALU.subtract))
                link(dve.tensor_tensor(far[:], pos[:], cell[:], ALU.subtract))
                link(dve.tensor_scalar(hat[:, 0], far[:], -1.0, 1.0, ALU.mult, ALU.add), False)
                link(dve.tensor_scalar(hat[:, 1], far[:], -1.0, 2.0, ALU.mult, ALU.add))
                link(dve.scalar_tensor_tensor(hat[:, 0], far[:], 1.0, hat[:, 0], ALU.add, ALU.min), False)
                link(dve.tensor_tensor(hat[:, 1], far[:], hat[:, 1], ALU.min))
                link(dve.tensor_scalar(hat[:], hat[:], 0.0, None, ALU.max))
                wv = wgt_all[:, image]
                for dy in range(2):
                    for dx in range(2):
                        link(dve.tensor_tensor(wv[:, :, dy + 2 * dx], hat[:, dy, :, 0], hat[:, dx, :, 1], ALU.mult),
                             False)
                link(dve.scalar_tensor_tensor(entry[:], cell[:, :, 0], float(W), cell[:, :, 1], ALU.mult, ALU.add))
                link(dve.tensor_scalar(idx_all[:, image], entry[:],
                                       float(HW * max(image - 1, 0)), None, ALU.add))
                assert done[0] == A_STEPS

            def window(h, ic):
                link, done = chain(corr_step, CORR_STEPS * ic + HALF_STEPS * h)
                dve.wait_ge(aligned, (RT - 1) * (4 * ic + 2 * h + 2))
                for c in (STEP_AT[("gram", 2 * h)], STEP_AT[("gram", 2 * h + 1)]):
                    dve.wait_ge(c_drained[BANK[c]], drains(ic, c) + 1)
                cv = corr[:, h].rearrange("p t y w -> p (t y) w")
                masked = picked[:].rearrange("p a b r -> p (a b r)")[:, 0:HT * KS * W]
                link(dve.tensor_tensor(masked.rearrange("p (a w) -> p a w", w=W), cv,
                                       band[:].unsqueeze(1).to_broadcast([P, HT * KS, W]), ALU.mult))
                link(dve.tensor_reduce(folded[:], masked.rearrange("p (a g r) -> p a r g", a=HT * KS, r=FOLD),
                                       AX.X, ALU.add))
                link(dve.tensor_tensor(picked[:], folded[:].unsqueeze(2).to_broadcast([P, HT * KS, KS, FOLD]),
                                       pick[:].unsqueeze(1).to_broadcast([P, HT * KS, KS, FOLD]), ALU.mult))
                gv = raw[:, h]
                link(dve.tensor_reduce(gv.rearrange("p t (y x) -> p (t y) x", x=KS), picked[:], AX.X, ALU.add))
                link(dve.tensor_tensor(gsq[:], gv, gv, ALU.mult))
                link(dve.tensor_reduce(nrm[:, h, 2, :], gsq[:], AX.X, ALU.add))
                dve.tensor_scalar(nrm[:, h, 0, :], nrm[:, h, 2, :], L1_EPS, None, ALU.add).then_inc(norm_asked, 1)

            def normalise(h, ic):
                link, done = chain(corr_step, CORR_STEPS * ic + HALF_STEPS * h + 6)
                total, root, tmp = (nrm[:, h, a, :] for a in range(3))
                dve.wait_ge(norm_asked, 2 * ic + h + 1)
                dve.wait_ge(norm_root, 2 * ic + h + 1)
                link(dve.reciprocal(tmp, root))
                link(dve.tensor_tensor(tmp, tmp, total, ALU.mult))
                link(dve.tensor_tensor(tmp, tmp, root, ALU.add))
                link(dve.reciprocal(root, tmp))
                if h:
                    dve.wait_ge(c_done, NC * ic + STEP_AT[("corrT", 0)] + 1)
                for p in range(3):
                    dve.scalar_tensor_tensor(gs[:, :, p, 0:NB], root.unsqueeze(2).to_broadcast([P, HT, NB]), 2.0,
                                             raw[:, h], ALU.mult, ALU.mult).then_inc(gs_done, 1)

            def body(items, ib, ic):
                for it in items:
                    if it[0] == "positions":
                        positions(it[1])
                    elif it[0] == "scale":
                        stage, w, _, u = SPLITS[it[1]]
                        dve.wait_ge(ld_late[u], 16 * len([s for s in SPLITS if s[3] == u]))
                        for m in range(KC):
                            sc = bn[:, 2, 2 + m:3 + m] if it[1] == 0 else prm[:, L3_S3 + m:L3_S3 + m + 1]
                            v = stage[:, m * P:(m + 1) * P]
                            dve.tensor_scalar(v, v, sc, None, ALU.mult).then_inc(scaled, 1)
                    elif it[0] == "split low" and it[1] == 7:
                        dve.wait_ge(corr_high, 3)
                        part = slice(PART, PART + NB)
                        dve.tensor_tensor(l1g[part], corr_stage[part], l1g[part].bitcast(fp32),
                                          ALU.subtract).then_inc(corr_low, 1)
                    elif it[0] == "split low":
                        stage, w, _, u = SPLITS[it[1]]
                        if it[1] < 2:
                            stage = bank[it[1]][:]
                        dve.wait_ge(high_done, it[1] + 1)
                        if w is l1w:
                            dve.wait_ge(a_step, A_STEPS * N)
                        dve.tensor_tensor(flat(w[1]), stage, flat(w[0]).bitcast(fp32),
                                          ALU.subtract).then_inc(low_done, 1)
                    elif it[0] == "take":
                        wait_past(dve, blended, UNITS * BLEND * ib)
                        wait_past(dve, ticked, 2 * UNITS * ib)
                        dve.tensor_copy(idx[:], idx_all[:, ib]).then_inc(taken, 1)
                        dve.tensor_copy(wgt[:], wgt_all[:, ib]).then_inc(taken, 1)
                        dve.wait_ge(taken, 2 * ib + 2)
                    elif it[0] == "blend":
                        _, u, pair = it
                        h, k = u // TAPS, u % TAPS
                        base = (UNITS * ib + u) * BLEND + 6 * pair
                        for corner in range(1, 4):
                            for tt in range(2):
                                t = 2 * pair + tt
                                w_ = wgt[:, (HT * h + t) * TAPS + k, corner:corner + 1]
                                g_ = patch[:, (HT * u + t) % SLOTS, corner, :]
                                o_ = samp[:, u % 2, t, :]
                                if corner == 1:
                                    dve.wait_ge(weighed, HT * (UNITS * ib + u) + t + 1)
                                else:
                                    dve.wait_ge(blended, base + 2 * corner + tt - 3)
                                dve.scalar_tensor_tensor(o_, g_, w_, o_, ALU.mult, ALU.add).then_inc(blended, 1)
                    elif it[0] == "out0":
                        _, h, m = it
                        n = 8 * ib + KC * h + m
                        dve.wait_ge(out0_done, n + 1)
                        r = (KC * h + m) % RES
                        uses = len(range(r, 2 * KC, RES))
                        dve.wait_ge(ld_res[r], 16 * (uses * ib + (KC * h + m) // RES + 1))
                        dve.scalar_tensor_tensor(res[:, r, :], bank[out_bank(h, m)][:],
                                                 prm[:, L0_S3 + m:L0_S3 + m + 1], res[:, r, :],
                                                 ALU.mult, ALU.add).then_inc(res_summed, 1)
                    elif it[0] == "outlow":
                        _, h, m = it
                        dve.wait_ge(x1_high, 8 * ib + KC * h + m + 1)
                        rows = slice(PADK + HR * h, PADK + HR * (h + 1))
                        value = res[:, (KC * h + m) % RES, :].rearrange("p (a b) -> p a b", b=W)
                        dve.tensor_tensor(x1[1][:, m, rows, :], value,
                                          x1[0][:, m, rows, :].bitcast(fp32), ALU.subtract).then_inc(x1_low, 1)
                    elif it[0] == "fine":
                        c = it[1]
                        value, high, low = split_parts(c)
                        dve.wait_ge(step_high, len(SPLIT_STEPS) * ic + HIGH_AT[c] + 1)
                        dve.tensor_tensor(low, value, high.bitcast(fp32), ALU.subtract).then_inc(fine_done, 1)
                    elif it[0] == "step":
                        c = it[1]
                        s = C_STEPS[c]
                        if s[:3] == ("expand", 3, 1):
                            slot_free(dve, ic, c)
                            dve.wait_ge(c_done, NC * ic + c + 1)
                            dve.tensor_scalar(slot(c), bank[BANK[c]][:], prm[:, L3_B3 + s[3]:L3_B3 + s[3] + 1], 0.0,
                                              ALU.add, ALU.max).then_inc(c_drained[BANK[c]], 1)
                        elif s[0] == "corrT":
                            dve.wait_ge(gsT_high, 2 * ic + s[1] + 1)
                            dve.tensor_tensor(gsT[2 * PART:3 * PART, :], bank[BANK[c]][2 * PART:3 * PART, :],
                                              gsT[2 * PART:3 * PART, :].bitcast(fp32), ALU.subtract)\
                               .then_inc(c_drained[BANK[c]], 1)
                    elif it[0] == "window":
                        window(it[1], ic)
                    elif it[0] == "normalise":
                        normalise(it[1], ic)

            body(PROLOGUE, 0, None)
            dve.sem_inc(fine_done, 1)
            with dve.Fori(1, N) as i:
                body(SCHEDULE, i, i - 1)
            body(EPILOGUE, None, N - 1)


def kernel(**inputs):
    import numpy as np
    import concourse.bacc as bacc
    from concourse import mybir
    from concourse.bass_utils import run_bass_kernel_spmd

    a = {k: np.asarray(v) for k, v in inputs.items()}

    def lay(w):
        return np.transpose(w.reshape(w.shape[0], w.shape[1], TAPS), (1, 2, 0))

    def chunks(w):
        return np.transpose(w.T.reshape(-1, P, w.shape[0]), (1, 0, 2))

    def cols(*names):
        return [a[n].reshape(-1, P).T for n in names]

    par = np.concatenate(
        cols("L0_conv_bn1_s", "L0_conv_bn1_b", "L0_conv_bn2_s", "L0_conv_bn2_b", "L0_conv_bn3_s", "L0_conv_bn3_b",
             "L1_conv_b")
        + cols(*[f"L2_conv_{v}{n}" for v in "gbmv" for n in (1, 2, 3)])
        + cols("L3_conv_scale1", "L3_conv_bias1", "L3_conv_scale2", "L3_conv_bias2", "L3_conv_scale3",
               "L3_conv_bias3"), axis=1)
    arrays = {
        "x": a["x"],
        "w1t": chunks(a["L0_conv_conv1_w"][:, :, 0, 0]),
        "offwt": lay(a["L0_conv_off_w"]).reshape(P, -1),
        "offb": np.broadcast_to(a["L0_conv_off_b"], (P, 2 * TAPS)),
        "w2t": lay(a["L0_conv_conv2_w"]).reshape(P, -1),
        "w3t": a["L0_conv_conv3_w"][:, :, 0, 0].T,
        "l1wt": chunks(a["L1_conv_W"][:, :C]),
        "l1gt": a["L1_conv_W"][:, C:].T,
        "l2w1t": chunks(a["L2_conv_w1"][:, :, 0, 0]),
        "l2w2t": lay(a["L2_conv_w2"]),
        "l2w3": a["L2_conv_w3"][:, :, 0, 0].reshape(KC, P, P).transpose(1, 0, 2),
        "l3w1t": chunks(a["L3_conv_w1"][:, :, 0, 0]),
        "l3w2t": lay(a["L3_conv_w2"]),
        "l3w3": a["L3_conv_w3"][:, :, 0, 0].reshape(KC, P, P).transpose(1, 0, 2),
        "par": par,
    }
    nc = bacc.Bacc("TRN2", target_bir_lowering=False, num_devices=1)
    given, args = {}, []
    for name, v in arrays.items():
        v = np.ascontiguousarray(v)
        given[f"in_{name}"] = v
        args.append(nc.dram_tensor(f"in_{name}", v.shape, mybir.dt.from_np(v.dtype), kind="ExternalInput").ap())
    out = nc.dram_tensor("out_y", (N, C, H, W), mybir.dt.float32, kind="ExternalOutput").ap()
    conv_seq_kernel(nc, *args, out)
    r = run_bass_kernel_spmd(nc, [given], core_ids=[0])
    return r.results[0]["out_y"]
```
